# Optimizing a Trainium2 kernel written in Bass

```python
import numpy as np
import jax
import jax.numpy as jnp

def _softmax(x, axis=-1):
    return jax.nn.softmax(x, axis=axis)

def _gelu(x):
    return jax.nn.gelu(x, approximate=True)

def _silu(x):
    return jax.nn.silu(x)

def _sigmoid(x):
    return jax.nn.sigmoid(x)

def _layernorm(x, axis=-1, eps=1e-05):
    m = jnp.mean(x, axis=axis, keepdims=True)
    v = jnp.var(x, axis=axis, keepdims=True)
    return (x - m) / jnp.sqrt(v + eps)

def _scatter_add(tgt, idx, src, axis=0):
    return tgt.at[idx].add(src)

def _segment_sum(src, seg, n):
    return jax.ops.segment_sum(src, seg, n)
kernel_name = 'mk_decoder_preln_d1_seqx_r8_921ffb'

def setup_inputs(seed: int=0):
    np.random.seed(seed)
    _w = jnp.asarray

    def _rec_inputs():
        import jax
        import jax.numpy as jnp
        _rk = jax.random.key(seed)
        x = -0.0003929 + 0.9999 * jax.random.normal(jax.random.fold_in(_rk, 1), (16, 256, 128), jnp.float32)
        _lenS = 256 - jax.random.randint(jax.random.fold_in(_rk, 7), (16,), 0, max(1, 256 // 4) + 1, jnp.int32)
        _lenS2 = 1601 - jax.random.randint(jax.random.fold_in(_rk, 8), (16,), 0, max(1, 1601 // 4) + 1, jnp.int32)
        _ctx_1024P = jax.random.normal(jax.random.fold_in(_rk, 11), (16, 16, 128), jnp.float32)
        _ctx_1024c = jax.random.dirichlet(jax.random.fold_in(_rk, 511), 0.3 * jnp.ones((16,), jnp.float32), (16, 1601))
        _ctx_1024t = jnp.einsum('bsk,bkd->bsd', _ctx_1024c, _ctx_1024P)
        _ctx_1024t = _ctx_1024t * jax.lax.rsqrt(jnp.mean(jnp.square(_ctx_1024t)) + 1e-12) * 0.953939
        ctx_1024 = 2.81802e-05 + 1.00001 * (_ctx_1024t + 0.3 * jax.random.normal(jax.random.fold_in(_rk, 611), (16, 1601, 128), jnp.float32))
        return (x, ctx_1024)
    x, ctx_1024 = _rec_inputs()

    def _L0_attn_setup():
        import jax, jax.numpy as jnp
        import numpy as np
        THETA = 10000.0

        def rope_rotate(x):
            T, C = (x.shape[-2], x.shape[-1])
            inv_freq = 1.0 / THETA ** (jnp.arange(0, C, 2, dtype=jnp.float32) / C)
            freqs = jnp.arange(T, dtype=jnp.float32)[:, None] * inv_freq[None, :]
            freqs = jnp.repeat(freqs, 2, axis=-1)
            cos, sin = (jnp.cos(freqs), jnp.sin(freqs))
            xp = x.reshape(x.shape[:-1] + (C // 2, 2))
            x_rot = jnp.stack((-xp[..., 1], xp[..., 0]), axis=-1).reshape(x.shape)
            return x * cos + x_rot * sin
        key = jax.random.key(seed)
        ks = jax.random.split(key, 5)
        B, T, C = (4, 256, 128)
        s = 1.0 / np.sqrt(C)
        return {'x': jax.random.normal(ks[0], (B, T, C), jnp.float32), 'Wq': jax.random.normal(ks[1], (C, C), jnp.float32) * s, 'bq': jnp.zeros((C,), jnp.float32), 'Wk': jax.random.normal(ks[2], (C, C), jnp.float32) * s, 'bk': jnp.zeros((C,), jnp.float32), 'Wv': jax.random.normal(ks[3], (C, C), jnp.float32) * s, 'bv': jnp.zeros((C,), jnp.float32), 'Wo': jax.random.normal(ks[4], (C, C), jnp.float32) * s, 'bo': jnp.zeros((C,), jnp.float32)}
    _L0_attn_all = _L0_attn_setup()
    _L0_attn_in = {k: v for k, v in _L0_attn_all.items() if k in ('Wq', 'bq', 'Wk', 'bk', 'Wv', 'bv', 'Wo', 'bo')}
    del _L0_attn_all

    def _L0_xattn_setup():
        import jax, jax.numpy as jnp
        import numpy as np
        B, S, H, P = (4, 512, 128, 10)
        key = jax.random.key(seed)
        k1, k2, k3, k4, k5 = jax.random.split(key, 5)
        return {'query': jax.random.normal(k1, (B, S, H), dtype=jnp.float32), 'key': jax.random.normal(k2, (B, S, H), dtype=jnp.float32), 'value': jax.random.normal(k3, (B, S, H), dtype=jnp.float32), 'prefix_k': jax.random.normal(k4, (P, H), dtype=jnp.float32), 'prefix_v': jax.random.normal(k5, (P, H), dtype=jnp.float32)}
    _L0_xattn_all = _L0_xattn_setup()
    _L0_xattn_in = {k: v for k, v in _L0_xattn_all.items() if k in ('prefix_k', 'prefix_v')}
    del _L0_xattn_all

    def _L0_ffn_setup():
        import jax, jax.numpy as jnp
        import numpy as np
        TOPK = 8
        NUM_EXPERTS = 64
        FFN = 384
        CAPACITY = 160

        def _swiglu(x, w1, w2):
            h = x @ w1.T
            x1, x2 = jnp.split(h, 2, axis=-1)
            return x1 * jax.nn.silu(x2) @ w2.T
        key = jax.random.key(seed)
        ks = jax.random.split(key, 6)
        B, S, H = (1, 64, 128)
        scale = 0.02
        return {'hidden_states': jax.random.normal(ks[0], (B, S, H), jnp.float32), 'wg': jax.random.normal(ks[1], (NUM_EXPERTS, H), jnp.float32) * scale, 'shared_w1': jax.random.normal(ks[2], (2 * FFN, H), jnp.float32) * scale, 'shared_w2': jax.random.normal(ks[3], (H, FFN), jnp.float32) * scale, 'expert_w1': jax.random.normal(ks[4], (NUM_EXPERTS, 2 * FFN, H), jnp.float32) * scale, 'expert_w2': jax.random.normal(ks[5], (NUM_EXPERTS, H, FFN), jnp.float32) * scale}
    _L0_ffn_all = _L0_ffn_setup()
    _L0_ffn_in = {k: v for k, v in _L0_ffn_all.items() if k in ('wg', 'shared_w1', 'shared_w2', 'expert_w1', 'expert_w2')}
    del _L0_ffn_all
    return {'x': x, 'ctx_1024': ctx_1024, 'L0_attn_Wq': _L0_attn_in['Wq'], 'L0_attn_bq': _L0_attn_in['bq'], 'L0_attn_Wk': _L0_attn_in['Wk'], 'L0_attn_bk': _L0_attn_in['bk'], 'L0_attn_Wv': _L0_attn_in['Wv'], 'L0_attn_bv': _L0_attn_in['bv'], 'L0_attn_Wo': _L0_attn_in['Wo'], 'L0_attn_bo': _L0_attn_in['bo'], 'L0_xattn_prefix_k': _L0_xattn_in['prefix_k'], 'L0_xattn_prefix_v': _L0_xattn_in['prefix_v'], 'L0_ffn_wg': _L0_ffn_in['wg'], 'L0_ffn_shared_w1': _L0_ffn_in['shared_w1'], 'L0_ffn_shared_w2': _L0_ffn_in['shared_w2'], 'L0_ffn_expert_w1': _L0_ffn_in['expert_w1'], 'L0_ffn_expert_w2': _L0_ffn_in['expert_w2']}

def reference(x, ctx_1024, L0_attn_Wq, L0_attn_bq, L0_attn_Wk, L0_attn_bk, L0_attn_Wv, L0_attn_bv, L0_attn_Wo, L0_attn_bo, L0_xattn_prefix_k, L0_xattn_prefix_v, L0_ffn_wg, L0_ffn_shared_w1, L0_ffn_shared_w2, L0_ffn_expert_w1, L0_ffn_expert_w2):
    import jax
    import jax.numpy as jnp

    def _L0_attn_ref(x, Wq, bq, Wk, bk, Wv, bv, Wo, bo):
        import jax, jax.numpy as jnp
        import numpy as np
        THETA = 10000.0

        def rope_rotate(x):
            T, C = (x.shape[-2], x.shape[-1])
            inv_freq = 1.0 / THETA ** (jnp.arange(0, C, 2, dtype=jnp.float32) / C)
            freqs = jnp.arange(T, dtype=jnp.float32)[:, None] * inv_freq[None, :]
            freqs = jnp.repeat(freqs, 2, axis=-1)
            cos, sin = (jnp.cos(freqs), jnp.sin(freqs))
            xp = x.reshape(x.shape[:-1] + (C // 2, 2))
            x_rot = jnp.stack((-xp[..., 1], xp[..., 0]), axis=-1).reshape(x.shape)
            return x * cos + x_rot * sin
        B, T, C = x.shape
        Q = rope_rotate(x @ Wq + bq)
        K = rope_rotate(x @ Wk + bk)
        V = x @ Wv + bv
        A = jnp.einsum('btc,bsc->bts', Q, K) / jnp.sqrt(jnp.float32(C))
        causal = jnp.tril(jnp.ones((T, T), dtype=bool))
        A = jnp.where(causal, A, -jnp.inf)
        P = jax.nn.softmax(A, axis=-1)
        out = jnp.einsum('bts,bsc->btc', P, V)
        return out @ Wo + bo

    def _L0_xattn_ref(query, key, value, prefix_k, prefix_v):
        import jax, jax.numpy as jnp
        import numpy as np
        B, S, H, P = (4, 512, 128, 10)
        b = query.shape[0]
        pk = jnp.broadcast_to(prefix_k[None], (b,) + prefix_k.shape)
        pv = jnp.broadcast_to(prefix_v[None], (b,) + prefix_v.shape)
        k_all = jnp.concatenate([pk, key], axis=1)
        v_all = jnp.concatenate([pv, value], axis=1)
        scores = jnp.einsum('bqh,bkh->bqk', query, k_all)
        attn = jax.nn.softmax(scores, axis=-1)
        return jnp.einsum('bqk,bkh->bqh', attn, v_all)

    def _L0_ffn_ref(hidden_states, wg, shared_w1, shared_w2, expert_w1, expert_w2):
        import jax, jax.numpy as jnp
        import numpy as np
        TOPK = 8
        NUM_EXPERTS = 64
        FFN = 384
        CAPACITY = 160

        def _swiglu(x, w1, w2):
            h = x @ w1.T
            x1, x2 = jnp.split(h, 2, axis=-1)
            return x1 * jax.nn.silu(x2) @ w2.T
        B, S, H = hidden_states.shape
        T = B * S
        x = hidden_states.reshape(T, H)
        shared_out = _swiglu(x, shared_w1, shared_w2)
        logits = x.astype(jnp.float32) @ wg.T
        gates = jax.nn.softmax(logits, axis=-1)
        w_topk, idx_topk = jax.lax.top_k(gates, TOPK)
        denom = jnp.maximum(w_topk.sum(-1, keepdims=True), jnp.finfo(jnp.float32).eps)
        w_topk = w_topk / denom
        A = T * TOPK
        flat_e = idx_topk.reshape(A)
        flat_w = w_topk.reshape(A)
        flat_t = jnp.repeat(jnp.arange(T), TOPK)
        order = jnp.argsort(flat_e)
        se, st, sw = (flat_e[order], flat_t[order], flat_w[order])
        counts = jnp.zeros(NUM_EXPERTS, jnp.int32).at[flat_e].add(1)
        starts = jnp.cumsum(counts) - counts
        rank = jnp.arange(A) - starts[se]
        valid = rank < CAPACITY
        buf = jnp.zeros((NUM_EXPERTS, CAPACITY, H), x.dtype).at[se, rank].set(x[st], mode='drop')
        h = jnp.einsum('ech,efh->ecf', buf, expert_w1)
        x1, x2 = jnp.split(h, 2, axis=-1)
        out = jnp.einsum('ecf,ehf->ech', x1 * jax.nn.silu(x2), expert_w2)
        y = out[se, jnp.clip(rank, 0, CAPACITY - 1)]
        y = jnp.where(valid[:, None], y * sw[:, None].astype(y.dtype), 0.0)
        combined = jnp.zeros((T, H), x.dtype).at[st].add(y)
        return (shared_out + combined).reshape(B, S, H)
    x = x + _L0_attn_ref(_layernorm(x, axis=-1), L0_attn_Wq, L0_attn_bq, L0_attn_Wk, L0_attn_bk, L0_attn_Wv, L0_attn_bv, L0_attn_Wo, L0_attn_bo)
    x = x + _L0_xattn_ref(_layernorm(x, axis=-1), ctx_1024, ctx_1024, L0_xattn_prefix_k, L0_xattn_prefix_v)
    x = x + _L0_ffn_ref(_layernorm(x, axis=-1), L0_ffn_wg, L0_ffn_shared_w1, L0_ffn_shared_w2, L0_ffn_expert_w1, L0_ffn_expert_w2)
    return x

_drawn_inputs = setup_inputs


def setup_inputs(seed=0):
    import zlib

    import numpy as np

    out = dict(_drawn_inputs(seed))
    spreads = {'L0_attn_bq': (0.0, 0.1),
     'L0_attn_bk': (0.0, 0.425),
     'L0_attn_bv': (0.0, 0.1),
     'L0_attn_bo': (0.0, 0.1)}
    factors = {'L0_ffn_wg': 8.0,
     'L0_ffn_shared_w1': 8.0,
     'L0_ffn_shared_w2': 8.0,
     'L0_ffn_expert_w1': 8.0,
     'L0_ffn_expert_w2': 8.0}
    for name, (base, spread) in spreads.items():
        noise = np.random.default_rng([zlib.crc32(name.encode()), seed]).standard_normal(out[name].shape)
        drawn = base * np.exp(spread * noise) if base else spread * noise
        out[name] = jnp.asarray(drawn.astype(out[name].dtype))
    for name, factor in factors.items():
        out[name] = (out[name] * factor).astype(out[name].dtype)
    return out
```

```python
from contextlib import ExitStack

import numpy as np

import concourse.bass as bass
from concourse import mybir

F32 = mybir.dt.float32
BF16 = mybir.dt.bfloat16
I32 = mybir.dt.int32
ALU = mybir.AluOpType
ACT = mybir.ActivationFunctionType
AX = mybir.AxisListType

P = 128
BATCHES, SEQ, DIM = 16, 256, 128
TOKENS = BATCHES * SEQ
TILES = TOKENS // P
CTX, PREFIX = 1601, 10
KEYS = CTX + PREFIX
KCH = -(-KEYS // P)
KLAST = KEYS - (KCH - 1) * P
CLAST = CTX - (KCH - 1) * P
EXPERTS, TOPK, CAP, FFN = 64, 8, 160, 384
FCH = FFN // P
SLOTS = EXPERTS * CAP
HALF = CAP // 2
SPARE = CAP
ZROWS = 76
ROW = DIM + EXPERTS + 1
EPS = 1e-5
GROUP = 4
STEP = 4
BANK = 512
FAR = 1.0e6
EW = 2 * FFN + FCH * DIM

C_ID, C_COS, C_SIN, C_MASK = 0, 128, 384, 640
C_TRI, C_BASE, C_END = 1024, 1152, 1216


def constants():
    c = np.zeros((P, C_END), np.float32)
    c[:, C_ID:C_ID + P] = np.eye(P)
    inv = (1.0 / np.float32(10000.0) ** (np.arange(0, DIM, 2, dtype=np.float32) / np.float32(DIM))).astype(np.float32)
    ang = np.repeat(np.arange(SEQ, dtype=np.float32)[:, None] * inv[None, :], 2, axis=-1)
    sign = np.where(np.arange(DIM) % 2 == 0, -1.0, 1.0).astype(np.float32)
    c[:, C_COS:C_COS + SEQ] = np.cos(ang).T
    c[:, C_SIN:C_SIN + SEQ] = np.sin(ang).T * sign[:, None]
    q = np.arange(P)[:, None]
    far = np.float32(-1e30)
    c[:, C_MASK:C_MASK + P] = np.where(np.arange(P)[None] <= q, 0, far)
    c[:, C_MASK + 2 * P:C_MASK + 3 * P] = c[:, C_MASK:C_MASK + P]
    c[:, C_TRI:C_TRI + P] = np.arange(P)[:, None] < np.arange(P)[None]
    c[:, C_BASE:C_BASE + EXPERTS] = np.arange(EXPERTS) * CAP + 1
    return c


def wait(eng, sem, value):
    if isinstance(value, int) and value <= 0:
        return
    eng.wait_ge(sem, value)


def wait_apart(eng, met, sem, value):
    if isinstance(value, int):
        return wait(eng, sem, value)
    value = eng.to_reg(value)
    eng.wait_ge(met, 1)
    eng.wait_ge(sem, value)


class Chain:

    def __init__(self, eng, sem, item, per):
        self.eng, self.sem, self.base, self.per, self.n = eng, sem, item * per, per, 0

    def __call__(self, instruction, met=None):
        instruction.then_inc(self.sem, 1)
        self.n += 1
        if met is not None:
            wait_apart(self.eng, met, self.sem, self.base + self.n)
        else:
            self.eng.wait_ge(self.sem, self.base + self.n)

    def end(self):
        assert self.n == self.per, (self.n, self.per)


def decoder_layer(nc, x, ctxT, ctxN, preT, preV, wqkvo, bcol, bo, wgT, sw, ew, cst, out):
    slots = nc.dram_tensor("slots", [SLOTS, ROW], F32, kind="Internal").ap()
    acc1 = nc.dram_tensor("acc1", [TOKENS + SPARE, DIM], F32, kind="Internal").ap()
    es = ExitStack()
    with es:
        def sb(name, shape, dt=F32):
            return es.enter_context(nc.sbuf_tensor(name, shape, dt))

        def sem(name):
            return es.enter_context(nc.semaphore(name))

        X = sb("X", [P, TILES, DIM])
        x3T = sb("x3T", [P, TOKENS])
        C = sb("C", [P, C_END])
        ident = C[:, C_ID:C_ID + P]
        W = sb("W", [P, 6, DIM])
        bias = sb("bias", [P, 5])
        bo_all = sb("bo_all", [P, DIM])
        WG = sb("WG", [P, EXPERTS])
        SW = sb("SW", [P, EW])
        mhalf = sb("mhalf", [P, 2])
        tri = sb("tri", [P, P], BF16)
        ones = sb("ones", [P, P], BF16)
        st1 = sb("st1", [P, 2 * GROUP, 6])
        mv1 = sb("mv1", [P, 2 * GROUP, 2])
        rs1 = sb("rs1", [P, 2 * GROUP])
        vv1 = sb("vv1", [P, 2 * GROUP])
        xn = sb("xn", [P, 2 * GROUP, DIM])
        xnT = sb("xnT", [P, GROUP, SEQ])
        rc = sb("rc", [P, 2, 2 * SEQ])
        rsn = sb("rsn", [P, 2, 2 * SEQ])
        qk = sb("qk", [P, GROUP, 2 * SEQ])
        v1 = sb("v1", [P, GROUP, SEQ])
        pr = sb("pr", [P, GROUP, 3 * P])
        nm1 = sb("nm1", [P, GROUP, 2])
        sm1 = sb("sm1", [P, GROUP, 2])
        ri1 = sb("ri1", [P, GROUP, 2])
        prT = sb("prT", [P, GROUP, 3 * P])
        oT = sb("oT", [P, GROUP, SEQ])
        KT = sb("KT", [P, 2, KEYS])
        V = sb("V", [P, 2, KCH, DIM])
        st2 = sb("st2", [P, 2, 6])
        mv2 = sb("mv2", [P, 2, 2])
        vv2 = sb("vv2", [P, 2, 2])
        rs2 = sb("rs2", [P, 2, 2])
        rtmp = sb("rtmp", [P, 2])
        vh = sb("vh", [P, 2])
        q2n = sb("q2n", [P, 2, DIM])
        q2T = sb("q2T", [P, 2, P])
        mx = sb("mx", [P, 2, 2])
        nmx = sb("nmx", [P, 2])
        pe2 = sb("pe2", [P, 2, KEYS])
        sm2 = sb("sm2", [P, 2])
        ri2 = sb("ri2", [P, 2])
        pT = sb("pT", [P, 2, KCH * P])
        st3 = sb("st3", [P, 2, 6])
        mv3 = sb("mv3", [P, 2, 2])
        rows = sb("rows", [P, STEP, ROW])
        x3s = sb("x3s", [P, 2, P])
        nlm = sb("nlm", [P, 2])
        gt = sb("gt", [P, 2, EXPERTS])
        gsum = sb("gsum", [P, 2])
        gri = sb("gri", [P, 2])
        top = sb("top", [P, 2, TOPK])
        left = sb("left", [P, 2, EXPERTS])
        tsum = sb("tsum", [P, 2])
        mask = sb("mask", [P, 2, EXPERTS], BF16)
        before = sb("before", [P, 2, EXPERTS], BF16)
        over = sb("over", [P, EXPERTS])
        slot = sb("slot", [P, EXPERTS])
        slot8 = sb("slot8", [P, TOPK])
        idx = sb("idx", [P, STEP, TOPK], I32)
        blank = sb("blank", [HALF, 2, ROW])
        pe2f = pe2[:, :, :].rearrange("p a b -> p (a b)")
        pTf = pT[:, :, :].rearrange("p a b -> p (a b)")
        sil3 = pe2f[:, 0:FCH * BANK].rearrange("p (j c) -> p j c", j=FCH)
        o3 = pe2f[:, FCH * BANK:FCH * BANK + 2 * BANK].rearrange("p (a n c) -> p a n c", a=2, n=4)
        g3 = pTf[:, 0:2 * FCH * BANK].rearrange("p (a j c) -> p a j c", a=2, j=FCH)
        EWT = sb("EWT", [P, STEP, EW])
        er = sb("er", [HALF, STEP, 2, ROW])
        tok4 = sb("tok4", [HALF, STEP, 2])
        gate4 = sb("gate4", [HALF, STEP, 2])
        xeT = sb("xeT", [P, 2, CAP])
        sil4 = sb("sil4", [P, 2, FCH * CAP])
        g4 = sb("g4", [P, 2, FCH * CAP])
        yT = sb("yT", [P, 2, CAP])
        yr = sb("yr", [HALF, STEP, 2, DIM])

        ps = es.enter_context(nc.psum_tensor("ps", [P, 8, BANK], F32))

        s_const = sem("s_const")
        s_kvfix = sem("s_kvfix")
        s_blank = sem("s_blank")
        s_fill = sem("s_fill")
        s_ready = sem("s_ready")
        s_poolc = sem("s_poolc")
        a_x = sem("a_x")
        a_stats = sem("a_stats")
        a_rstd = sem("a_rstd")
        a_xn = sem("a_xn")
        a_xnTp = sem("a_xnTp")
        a_xnT = sem("a_xnT")
        a_qkv = sem("a_qkv")
        a_rope = sem("a_rope")
        a_qk = sem("a_qk")
        a_v = sem("a_v")
        a_sc = sem("a_sc")
        a_max = sem("a_max")
        a_exp = sem("a_exp")
        a_prob = sem("a_prob")
        a_prTp = sem("a_prTp")
        a_prT = sem("a_prT")
        a_oTp = sem("a_oTp")
        a_oT = sem("a_oT")
        a_outp = sem("a_outp")
        a_x1 = sem("a_x1")
        a_c1, a_c2, a_c3 = sem("a_c1"), sem("a_c2"), sem("a_c3")
        k_in = [sem("k_in0"), sem("k_in1")]
        v_in = [sem("v_in0"), sem("v_in1")]
        b_q2n = sem("b_q2n")
        b_q2Tp = sem("b_q2Tp")
        b_q2T = sem("b_q2T")
        b_sc = sem("b_sc")
        b_max = sem("b_max")
        b_exp = sem("b_exp")
        b_pTp = sem("b_pTp")
        b_pTa = sem("b_pTa")
        b_pTb = sem("b_pTb")
        b_pTd = sem("b_pTd")
        b_pv = sem("b_pv")
        b_x2 = sem("b_x2")
        b_x3n = sem("b_x3n")
        b_x3Tp = sem("b_x3Tp")
        b_x3T = sem("b_x3T")
        b_lg = sem("b_lg")
        b_lmax = sem("b_lmax")
        b_lexp = sem("b_lexp")
        b_mask = sem("b_mask")
        b_rank = sem("b_rank")
        b_rkd = sem("b_rkd")
        b_idx = sem("b_idx")
        b_scat = [sem(f"b_scat{i}") for i in range(STEP)]
        c_ln2, c_x2, c_rs, c_rt, c_sl, c_mx = (sem(n) for n in ("c_ln2", "c_x2", "c_rs", "c_rt", "c_sl", "c_mx"))
        d_gate = sem("d_gate")
        d_up = sem("d_up")
        d_sil = sem("d_sil")
        d_g = sem("d_g")
        d_y = sem("d_y")
        d_o = sem("d_o")
        d_st = [sem("d_st0"), sem("d_st1")]
        w_in = [sem(f"w_in{i}") for i in range(STEP)]
        r_in = [sem(f"r_in{i}") for i in range(STEP)]
        e_xTp = sem("e_xTp")
        e_xT = sem("e_xT")
        e_row = sem("e_row")
        e_h = sem("e_h")
        e_sil = sem("e_sil")
        e_g = sem("e_g")
        e_yTp = sem("e_yTp")
        e_yT = sem("e_yT")
        e_yp = sem("e_yp")
        e_y = sem("e_y")
        e_add = [sem("e_add0"), sem("e_add1")]
        f_add = sem("f_add")

        block = es.enter_context(nc.Block())

        @block.sync
        def _(sp):
            half = TILES // 2
            xt = x.rearrange("(n p) c -> p n c", p=P)
            sp.dma_start(X[:, 0:8, :], xt[:, 0:8, :]).then_inc(s_const, 16)
            sp.dma_start(C[:, :], cst).then_inc(s_const, 16)
            sp.dma_start(W[:, :, :], wqkvo).then_inc(s_const, 16)
            sp.dma_start(bias[:, :], bcol).then_inc(s_const, 16)
            sp.dma_start(bo_all[:, :], bo.to_broadcast([P, DIM])).then_inc(s_const, 16)
            sp.dma_start(X[:, 8:TILES, :], xt[:, 8:TILES, :]).then_inc(s_const, 16)
            sp.dma_start(WG[:, :], wgT).then_inc(s_const, 16)
            sp.dma_start(SW[:, :], sw).then_inc(s_const, 16)
            for p in range(2):
                sp.dma_start(KT[:, p, CTX:KEYS], preT).then_inc(s_kvfix, 16)
                sp.dma_start(V[CLAST:KLAST, p, KCH - 1, :], preV).then_inc(s_kvfix, 16)

            def load_ctx(b, p, after):
                if after:
                    sp.wait_ge(b_sc, 4 * (b - 1))
                sp.dma_start(KT[:, p, 0:CTX], ctxT[b]).then_inc(k_in[p], 16)
                if after:
                    sp.wait_ge(b_pv, 2 * (b - 1))
                whole = (KCH - 1) * P
                src = ctxN[b]
                sp.dma_start(V[:, p, 0:KCH - 1, :], src[0:whole, :].rearrange("(n p) c -> p n c", p=P))\
                    .then_inc(v_in[p], 16)
                sp.dma_start(V[0:CLAST, p, KCH - 1, :], src[whole:CTX, :]).then_inc(v_in[p], 16)

            load_ctx(0, 0, False)
            load_ctx(1, 1, False)
            sp.wait_ge(s_blank, 1)
            for h in range(2):
                sp.dma_start(slots.rearrange("(n h p) c -> h p n c", h=2, p=HALF)[h],
                             blank[:, h, :].unsqueeze(1).to_broadcast([HALF, EXPERTS, ROW])).then_inc(s_fill, 16)
            rest = (TOKENS + SPARE) // ZROWS
            sp.dma_start(acc1.rearrange("(n p) c -> p n c", p=ZROWS),
                         blank[0:ZROWS, 0, 0:DIM].unsqueeze(1).to_broadcast([ZROWS, rest, DIM])).then_inc(s_fill, 16)
            sp.dma_start(out[TOKENS:TOKENS + SPARE, :].rearrange("(h p) c -> p h c", h=2), blank[:, :, 0:DIM])\
                .then_inc(s_fill, 16)
            with sp.Fori(1, BATCHES // 2) as k:
                for p in range(2):
                    load_ctx(2 * k + p, p, True)

            def load_expert(e, i, after):
                if after:
                    sp.wait_ge(e_yTp, e - STEP + 1)
                sp.dma_start(EWT[:, i, :], ew[e]).then_inc(w_in[i], 16)

            def load_rows(e, i):
                sp.dma_start(er[:, i, :, :], slots[bass.ds(e * CAP, CAP), :].rearrange("(h p) c -> p h c", h=2))\
                    .then_inc(r_in[i], 16)

            for i in range(STEP):
                load_expert(i, i, False)
            ov = out[0:TOKENS, :].rearrange("(n p) c -> p n c", p=P)
            with sp.Fori(0, TOKENS // BANK // 2) as k:
                for p in range(2):
                    sp.wait_ge(d_o, 2 * k + p + 1)
                    sp.dma_start(ov[:, bass.ds(8 * k + 4 * p, 4), :], o3[:, p, :, :]).then_inc(d_st[p], 16)
            for i in range(STEP):
                sp.wait_ge(b_scat[i], 16 * TOPK * TILES // STEP)
            for i in range(STEP):
                load_rows(i, i)
            with sp.Fori(1, EXPERTS // STEP) as k:
                for i in range(STEP):
                    load_expert(k * STEP + i, i, True)
                    sp.wait_ge(e_xTp, (k - 1) * STEP + i + 1)
                    sp.wait_ge(e_row, (k - 1) * STEP + i + 1)
                    load_rows(k * STEP + i, i)

        @block.gpsimd
        def _(pool):
            last_slot, last_row = pool.to_reg(SLOTS - 1), pool.to_reg(TOKENS + SPARE - 1)
            pool.memset(ones[:, :], 1.0)
            pool.memset(mhalf[:, :], -0.5)
            pool.memset(vv2[:, :, :], 1.0)
            pool.memset(before[:, :, :], 0.0).then_inc(s_poolc, 1)
            pool.memset(blank[:, :, :], 0.0).then_inc(s_poolc, 1)
            pool.wait_ge(s_poolc, 2)
            pool.iota(blank[:, :, ROW - 1:ROW].bitcast(I32), pattern=[[HALF, 2], [0, 1]], base=TOKENS,
                      channel_multiplier=1).then_inc(s_blank, 1)
            for i in range(STEP):
                pool.iota(rows[:, i, ROW - 1:ROW].bitcast(I32), pattern=[[0, 1]], base=P * (i - STEP),
                          channel_multiplier=1).then_inc(s_poolc, 1)
            pool.wait_ge(s_const, 8 * 16)

            with pool.Fori(0, BATCHES // GROUP) as g:
                for j in range(GROUP):
                    b = g * GROUP + j
                    pool.wait_ge(a_stats, b + 1)
                    pool.tensor_tensor(rs1[:, 2 * j:2 * j + 2], vv1[:, 2 * j:2 * j + 2], mhalf[:, :], ALU.pow)\
                        .then_inc(a_rstd, 1)
                for j in range(GROUP):
                    b = g * GROUP + j
                    pool.wait_ge(a_xn, b + 1)
                    xb = X[:, bass.ds(2 * b, 2), :]
                    pool.tensor_tensor(xb, xb, bo_all[:, :].unsqueeze(1).to_broadcast([P, 2, DIM]), ALU.add)\
                        .then_inc(a_x, 1)
                    pool.wait_ge(a_rope, b + 1)
                    pool.tensor_tensor(qk[:, j, :], rc[:, j % 2, :], rsn[:, j % 2, :], ALU.add).then_inc(a_qk, 1)

            def scatter(t, r, ks):
                wait_apart(pool, s_blank, b_idx, t + 1)
                for k in ks:
                    pool.indirect_dma_start(slots, bass.IndirectOffsetOnAxis(ap=idx[:, r, k:k + 1], axis=0),
                                            rows[:, r, :], None, bounds_check=last_slot, oob_is_err=False)\
                        .then_inc(b_scat[r], 16)

            def period(t, r, k, lo, hi):
                if lo <= 4 <= hi:
                    scatter(t - 4, r, range(TOPK))

            pool.wait_ge(s_fill, 64)
            periods(pool, period)

            def add(e, i, k):
                if not (isinstance(e, int) and e < 2):
                    pool.wait_ge(e_add[i % 2], 32 * (2 * k + i // 2))
                wait_apart(pool, s_blank, e_y, e + 1)
                for h in range(2):
                    acc = out if i % 2 == 0 else acc1
                    pool.indirect_dma_start(
                        acc, bass.IndirectOffsetOnAxis(ap=tok4[:, i, h:h + 1].bitcast(I32), axis=0),
                        yr[:, i, h, :], None, bounds_check=last_row, oob_is_err=True,
                        compute_op=ALU.add).then_inc(e_add[i % 2], 16)

            for p in range(2):
                pool.wait_ge(d_st[p], 16 * (TOKENS // BANK // 2))
            for i in range(STEP):
                add(i, i, 0)
            with pool.Fori(1, EXPERTS // STEP) as k:
                for i in range(STEP):
                    add(k * STEP + i, i, k)
            for p in range(2):
                pool.wait_ge(e_add[p], 32 * (EXPERTS // 2))
            pool.dma_start(out[0:TOKENS, :].rearrange("(p r) c -> p (r c)", p=P),
                           acc1[0:TOKENS, :].rearrange("(p r) c -> p (r c)", p=P),
                           accum_op=ALU.add, max_dma_last_dim=4096).then_inc(f_add, 16)
            pool.wait_ge(f_add, 16)

        @block.tensor
        def _(pe):
            pe.wait_ge(s_const, 8 * 16)
            mm, tr = pe.matmul, pe.transpose
            with pe.Fori(0, BATCHES // GROUP) as g:
                for j in range(GROUP):
                    b = g * GROUP + j
                    pe.wait_ge(a_xn, b + 1)
                    if j < 2:
                        pe.wait_ge(a_x1, b - j)
                    else:
                        pe.wait_ge(a_xnT, b - 1)
                    tr(ps[:, j % 2, 0:P], xn[:, 2 * j, :], ident)
                    tr(ps[:, j % 2, P:2 * P], xn[:, 2 * j + 1, :], ident).then_inc(a_xnTp, 1)
                for j in range(GROUP):
                    b = g * GROUP + j
                    pe.wait_ge(a_xnT, b + 1)
                    if j >= 2:
                        pe.wait_ge(a_rope, b - 1)
                        pe.wait_ge(a_v, b - 1)
                    for w, (bank, col) in enumerate([(2, 0), (4, 0), (2, SEQ), (4, SEQ)]):
                        mm(ps[:, bank + j % 2, col:col + SEQ], W[:, w, :], xnT[:, j, :], start=True, stop=True)
                    for i in range(2):
                        last = mm(ps[:, 6 + j % 2, i * P:(i + 1) * P], xnT[:, j, i * P:(i + 1) * P], W[:, 4, :],
                                  start=True, stop=True)
                    last.then_inc(a_qkv, 1)
                for j in range(GROUP):
                    b = g * GROUP + j
                    pe.wait_ge(a_qk, b + 1)
                    if j == 0:
                        pe.wait_ge(a_rope, b + GROUP)
                    if j >= 2:
                        pe.wait_ge(a_max, b - 1)
                    mm(ps[:, 2 + j % 2, 0:P], qk[:, j, 0:P], qk[:, j, SEQ:SEQ + P], start=True, stop=True)
                    mm(ps[:, 2 + j % 2, P:3 * P], qk[:, j, P:2 * P], qk[:, j, SEQ:2 * SEQ], start=True,
                       stop=True).then_inc(a_sc, 1)
                for j in range(GROUP):
                    b = g * GROUP + j
                    pe.wait_ge(a_prob, b + 1)
                    if j >= 2:
                        pe.wait_ge(a_prT, b - 1)
                    for i in range(3):
                        last = tr(ps[:, 4 + j % 2, i * P:(i + 1) * P], pr[:, j, i * P:(i + 1) * P], ident)
                    last.then_inc(a_prTp, 1)
                for j in range(GROUP):
                    b = g * GROUP + j
                    pe.wait_ge(a_prT, b + 1)
                    if j == 0:
                        pe.wait_ge(a_v, b + GROUP)
                    if j >= 2:
                        pe.wait_ge(a_oT, b - 1)
                    o = ps[:, 6 + j % 2, :]
                    mm(o[:, 0:SEQ], v1[:, j, 0:P], prT[:, j, 0:SEQ], start=True, stop=False)
                    mm(o[:, P:SEQ], v1[:, j, P:SEQ], prT[:, j, SEQ:3 * P], start=False, stop=True).then_inc(a_oTp, 1)
                for j in range(GROUP):
                    b = g * GROUP + j
                    pe.wait_ge(a_oT, b + 1)
                    if j >= 2:
                        pe.wait_ge(a_x1, b - 1)
                    for i in range(2):
                        last = mm(ps[:, j % 2, i * P:(i + 1) * P], oT[:, j, i * P:(i + 1) * P], W[:, 5, :],
                                  start=True, stop=True)
                    last.then_inc(a_outp, 1)

            def period(t, r, k, lo, hi):
                p = r % 2
                o = 1 - p
                batch = (r // 2) % 2
                if lo <= 0 <= hi:
                    wait(pe, b_q2T, t + 1)
                    wait(pe, b_exp, t)
                    if p == 0:
                        pe.wait_ge(k_in[batch], 16 * (k + 1))
                    for i in range(4):
                        c0, c1 = i * BANK, min(KEYS, (i + 1) * BANK)
                        last = mm(ps[:, i, 0:c1 - c0], q2T[:, p, :], KT[:, batch, c0:c1], start=True, stop=True)
                        if i % 2:
                            last.then_inc(b_sc, 1)
                if lo <= 3 <= hi:
                    wait(pe, b_mask, t - 2)
                    wait(pe, b_lexp, t - 2)
                    mm(ps[:, 7, 0:EXPERTS], tri[:, :], mask[:, o, :], start=True, stop=False)
                    mm(ps[:, 7, 0:EXPERTS], ones[:, :], before[:, o, :], start=False, stop=True).then_inc(b_rank, 1)

                def transposed(gr):
                    wait(pe, b_exp, t)
                    if gr == 1:
                        wait(pe, b_pTd, 2 * (t - 1))
                    if gr == 2:
                        wait(pe, b_pTa, t)
                    if gr == 3:
                        wait(pe, b_pTb, t)
                    for n in range(4 * gr, min(KCH, 4 * gr + 4)):
                        w = P if n < KCH - 1 else KLAST
                        last = tr(ps[0:w, 4 + gr % 2, (n % 4) * P:(n % 4 + 1) * P], pe2[:, o, n * P:n * P + w], ident)
                    last.then_inc(b_pTp, 1)

                def values(n0, n1):
                    for n in range(n0, n1):
                        w = P if n < KCH - 1 else KLAST
                        last = mm(ps[:, 6, 0:DIM], pT[0:w, o, n * P:(n + 1) * P], V[0:w, vb, n, :],
                                  start=(n == 0), stop=(n == KCH - 1))
                    return last

                vb = (((r + STEP - 1) % STEP) // 2) % 2
                if lo <= 1 <= hi:
                    transposed(0)
                    transposed(1)
                if lo <= 2 <= hi:
                    wait(pe, b_x3n, t - 1)
                    wait(pe, b_rkd, t - 2)
                    tr(ps[:, 7, 0:P], rows[:, (r + 2) % STEP, 0:DIM], ident).then_inc(b_x3Tp, 1)
                if lo <= 1 <= hi:
                    transposed(2)
                    transposed(3)
                    wait(pe, b_x2, t - 1)
                    if o == 0:
                        pe.wait_ge(v_in[vb], 32 * (k + 1))
                    wait(pe, b_pTa, t)
                    wait(pe, b_pTb, t)
                    values(0, 8)
                if lo <= -1 <= hi:
                    wait(pe, b_q2n, t + 2)
                    if lo <= 1 <= hi:
                        wait(pe, b_pTd, 2 * t - 1)
                    tr(ps[:, 4, 0:P], q2n[:, o, :], ident).then_inc(b_q2Tp, 1)
                if lo <= 2 <= hi:
                    wait(pe, b_x3T, t - 1)
                    mm(ps[:, 7, 0:EXPERTS], x3s[:, p, :], WG[:, :], start=True, stop=True).then_inc(b_lg, 1)
                if lo <= 1 <= hi:
                    wait(pe, b_pTd, 2 * t)
                    values(8, KCH).then_inc(b_pv, 1)

            pe.wait_ge(a_x1, BATCHES)
            pe.wait_ge(s_kvfix, 64)
            pe.wait_ge(s_ready, 1)
            pe.wait_ge(s_poolc, 2)
            periods(pe, period)

            def up3(c, p):
                for j in range(FCH):
                    if not (isinstance(c, int) and c == 0):
                        pe.wait_ge(d_g, 3 * c - FCH + j + 1)
                    for bank, f, s in ((3 + j, FFN + j * P, d_gate), (j, j * P, d_up)):
                        mm(ps[:, bank, :], SW[:, f:f + P], x3T[:, bass.ds(c * BANK, BANK)],
                           start=True, stop=True).then_inc(s, 1)

            def down3(c, p):
                pe.wait_ge(d_g, 3 * c + 3)
                if not (isinstance(c, int) and c < 2):
                    pe.wait_ge(d_o, c - 1)
                for i in range(4):
                    for j in range(FCH):
                        last = mm(ps[:, 6 + p, i * P:(i + 1) * P], g3[:, p, j, i * P:(i + 1) * P],
                                  SW[:, 2 * FFN + j * DIM:2 * FFN + (j + 1) * DIM],
                                  start=(j == 0), stop=(j == FCH - 1))
                last.then_inc(d_y, 1)

            pe.wait_ge(b_x3T, TILES)
            pe.wait_ge(b_lexp, TILES)
            pe.wait_ge(b_rkd, TILES)
            up3(0, 0)
            up3(1, 1)
            down3(0, 0)
            with pe.Fori(1, TOKENS // BANK // 2) as k:
                for p in range(2):
                    up3(2 * k + p, p)
                    down3(2 * k + p - 1, 1 - p)
            down3(TOKENS // BANK - 1, 1)

            def step(e, i, k, lo, hi):
                p = i % 2
                if lo <= 0 <= hi:
                    pe.wait_ge(e_xT, e + 1)
                    pe.wait_ge(w_in[i], 16 * (k + 1))
                    if not (isinstance(e, int) and e < 2):
                        pe.wait_ge(e_g, e - 1)
                    for f0, bank in ((FFN, 3), (0, 1)):
                        for j in range(FCH):
                            last = mm(ps[:, bank + p, j * CAP:(j + 1) * CAP], EWT[:, i, f0 + j * P:f0 + (j + 1) * P],
                                      xeT[:, p, :], start=True, stop=True)
                        last.then_inc(e_h, 1)
                if lo <= 1 <= hi:
                    pe.wait_ge(e_g, e)
                    if not (isinstance(e, int) and e < 2):
                        pe.wait_ge(e_yT, e - 1)
                    w = EWT[:, (i - 1) % STEP, 2 * FFN:]
                    for j in range(FCH):
                        last = mm(ps[:, 5, 0:CAP], w[:, j * DIM:(j + 1) * DIM], g4[:, 1 - p, j * CAP:(j + 1) * CAP],
                                  start=(j == 0), stop=(j == FCH - 1))
                    last.then_inc(e_yTp, 1)
                if lo <= 2 <= hi:
                    pe.wait_ge(e_yT, e - 1)
                    if not (isinstance(e, int) and e < 3):
                        pe.wait_ge(e_y, e - 2)
                    for h in range(2):
                        last = tr(ps[0:HALF, 6, h * P:(h + 1) * P], yT[:, p, h * HALF:(h + 1) * HALF], ident)
                    last.then_inc(e_yp, 1)
                if lo <= -1 <= hi:
                    i1 = (i + 1) % STEP
                    pe.wait_ge(r_in[i1], 16 * (k + 1 + (i + 1) // STEP))
                    if not (isinstance(e, int) and e < 0):
                        pe.wait_ge(e_xT, e + 1)
                    for h in range(2):
                        last = tr(ps[:, 0, h * HALF:(h + 1) * HALF], er[:, i1, h, 0:DIM], ident[0:HALF, 0:HALF])
                    last.then_inc(e_xTp, 1)

            pe.wait_ge(d_o, TOKENS // BANK)
            steps(pe, step)

        @block.scalar
        def _(act):
            act.wait_ge(s_const, 8 * 16)
            with act.Fori(0, BATCHES // GROUP) as g:
                for j in range(GROUP):
                    b = g * GROUP + j
                    act.wait_ge(a_xnTp, b + 1)
                    act.activation(xnT[:, j, :], ps[:, j % 2, 0:SEQ], ACT.Copy).then_inc(a_xnT, 1)
                for j in range(GROUP):
                    b = g * GROUP + j
                    act.wait_ge(a_qkv, b + 1)
                    act.activation(v1[:, j, :], ps[:, 6 + j % 2, 0:SEQ], ACT.Copy).then_inc(a_v, 1)
                for j in range(GROUP):
                    b = g * GROUP + j
                    act.wait_ge(a_max, b + 1)
                    for i, (c0, c1) in enumerate(((0, P), (P, 3 * P))):
                        last = act.activation(pr[:, j, c0:c1], pr[:, j, c0:c1], ACT.Exp, bias=nm1[:, j, i:i + 1],
                                              accum_out=sm1[:, j, i:i + 1])
                    last.then_inc(a_exp, 1)
                for j in range(GROUP):
                    b = g * GROUP + j
                    act.wait_ge(a_prTp, b + 1)
                    act.activation(prT[:, j, :], ps[:, 4 + j % 2, 0:3 * P], ACT.Copy).then_inc(a_prT, 1)
                for j in range(GROUP):
                    b = g * GROUP + j
                    act.wait_ge(a_oTp, b + 1)
                    act.activation(oT[:, j, :], ps[:, 6 + j % 2, 0:SEQ], ACT.Identity, bias=bias[:, 4:5])\
                        .then_inc(a_oT, 1)

            def period(t, r, k, lo, hi):
                p, o = r % 2, 1 - r % 2
                if lo <= 1 <= hi:
                    for gr, s in ((0, b_pTa), (1, b_pTb)):
                        wait(act, b_pTp, 4 * (t - 1) + gr + 1)
                        wait(act, b_pv, t - 2)
                        act.activation(pT[:, o, gr * BANK:(gr + 1) * BANK], ps[:, 4 + gr, :], ACT.Copy).then_inc(s, 1)
                if lo <= 2 <= hi:
                    wait(act, b_x3Tp, t - 1)
                    act.activation(x3s[:, p, :], ps[:, 7, 0:P], ACT.Copy)
                    act.activation(x3T[:, bass.ds((t - 2) * P, P)], ps[:, 7, 0:P], ACT.Copy).then_inc(b_x3T, 1)
                if lo <= 0 <= hi:
                    wait(act, b_max, t + 1)
                    wait(act, b_pTp, 4 * (t - 1))
                    act.activation(pe2[:, p, :], ps[:, 0:4, :].rearrange("p a b -> p (a b)")[:, 0:KEYS], ACT.Exp,
                                   bias=nmx[:, p:p + 1], accum_out=sm2[:, p:p + 1]).then_inc(b_exp, 1)
                if lo <= -1 <= hi:
                    wait(act, b_q2Tp, t + 2)
                    act.activation(q2T[:, o, :], ps[:, 4, 0:P], ACT.Copy).then_inc(b_q2T, 1)
                if lo <= 2 <= hi:
                    wait(act, b_lmax, t - 1)
                    act.activation(gt[:, p, :], ps[:, 7, 0:EXPERTS], ACT.Exp, bias=nlm[:, p:p + 1],
                                   accum_out=gsum[:, p:p + 1]).then_inc(b_lexp, 1)

            periods(act, period)

            def silu3(c):
                for j in range(FCH):
                    act.wait_ge(d_gate, 3 * c + j + 1)
                    if not (isinstance(c, int) and c == 0):
                        act.wait_ge(d_g, 3 * c - FCH + j + 1)
                    act.activation(sil3[:, j, :], ps[:, 3 + j, :], ACT.Silu).then_inc(d_sil, 1)

            silu3(0)
            with act.Fori(1, TOKENS // BANK) as c:
                silu3(c)

            def step(e, i, k, lo, hi):
                p = i % 2
                if lo <= 0 <= hi:
                    act.wait_ge(e_h, 2 * e + 1)
                    act.activation(sil4[:, p, :], ps[:, 3 + p, 0:FCH * CAP], ACT.Silu).then_inc(e_sil, 1)
                if lo <= 1 <= hi:
                    act.wait_ge(e_yTp, e)
                    if not (isinstance(e, int) and e < 3):
                        act.wait_ge(e_yp, e - 2)
                    act.activation(yT[:, 1 - p, :], ps[:, 5, 0:CAP], ACT.Copy).then_inc(e_yT, 1)
                if lo <= -1 <= hi:
                    act.wait_ge(e_xTp, e + 2)
                    act.activation(xeT[:, 1 - p, :], ps[:, 0, 0:CAP], ACT.Copy).then_inc(e_xT, 1)

            steps(act, step)

        @block.vector
        def _(dve):
            def tile_of(t):
                return X[:, bass.ds(t, 1), :].rearrange("p a c -> p (a c)")

            dve.wait_ge(s_const, 8 * 16)
            dve.tensor_copy(tri[:, :], C[:, C_TRI:C_TRI + P]).then_inc(s_ready, 1)
            dve.wait_ge(s_poolc, 2 + STEP)
            with dve.Fori(0, BATCHES // GROUP) as g:
                for j in range(GROUP):
                    b = g * GROUP + j
                    ch = Chain(dve, a_c1, b, 2)
                    for i in range(2):
                        last = dve.bn_stats(st1[:, 2 * j + i, :], tile_of(2 * b + i))
                    ch(last, s_ready)
                    for i in range(2):
                        last = dve.bn_aggr(mv1[:, 2 * j + i, :], st1[:, 2 * j + i, :])
                    ch(last)
                    ch.end()
                    dve.tensor_scalar(vv1[:, 2 * j:2 * j + 2], mv1[:, 2 * j:2 * j + 2, 1], EPS, None, ALU.add)\
                        .then_inc(a_stats, 1)
                for j in range(GROUP):
                    b = g * GROUP + j
                    dve.wait_ge(a_rstd, b + 1)
                    for i in range(2):
                        n = 2 * j + i
                        last = dve.tensor_scalar(xn[:, n, :], tile_of(2 * b + i),
                                                 mv1[:, n, 0:1], rs1[:, n:n + 1], ALU.subtract, ALU.mult)
                    last.then_inc(a_xn, 1)
                for j in range(GROUP):
                    b = g * GROUP + j
                    dve.wait_ge(a_qkv, b + 1)
                    if j >= 2:
                        dve.wait_ge(a_qk, b - 1)
                    for w in range(2):
                        cols = slice(w * SEQ, (w + 1) * SEQ)
                        dve.scalar_tensor_tensor(rc[:, j % 2, cols], ps[:, 2 + j % 2, cols], bias[:, 2 * w:2 * w + 1],
                                                 C[:, C_COS:C_COS + SEQ], ALU.add, ALU.mult)
                        last = dve.scalar_tensor_tensor(rsn[:, j % 2, cols], ps[:, 4 + j % 2, cols],
                                                        bias[:, 2 * w + 1:2 * w + 2], C[:, C_SIN:C_SIN + SEQ],
                                                        ALU.add, ALU.mult)
                    last.then_inc(a_rope, 1)
                for j in range(GROUP):
                    b = g * GROUP + j
                    dve.wait_ge(a_sc, b + 1)
                    ch = Chain(dve, a_c2, b, 1)
                    ch(dve.scalar_tensor_tensor(pr[:, j, :], ps[:, 2 + j % 2, 0:3 * P], float(DIM) ** -0.5,
                                                C[:, C_MASK:C_MASK + 3 * P], ALU.mult, ALU.add))
                    ch.end()
                    dve.tensor_reduce(nm1[:, j, 0:1], pr[:, j, 0:P], AX.X, ALU.max, negate=True)
                    dve.tensor_reduce(nm1[:, j, 1:2], pr[:, j, P:3 * P], AX.X, ALU.max, negate=True).then_inc(a_max, 1)
                for j in range(GROUP):
                    b = g * GROUP + j
                    dve.wait_ge(a_exp, b + 1)
                    ch = Chain(dve, a_c3, b, 1)
                    ch(dve.reciprocal(ri1[:, j, :], sm1[:, j, :]))
                    ch.end()
                    dve.tensor_scalar(pr[:, j, 0:P], pr[:, j, 0:P], ri1[:, j, 0:1], None, ALU.mult)
                    dve.tensor_scalar(pr[:, j, P:3 * P], pr[:, j, P:3 * P], ri1[:, j, 1:2], None, ALU.mult)\
                        .then_inc(a_prob, 1)
                for j in range(GROUP):
                    b = g * GROUP + j
                    dve.wait_ge(a_outp, b + 1)
                    dve.wait_ge(a_x, b + 1)
                    xb = X[:, bass.ds(2 * b, 2), :].rearrange("p a c -> p (a c)")
                    dve.tensor_tensor(xb, ps[:, j % 2, 0:SEQ], xb, ALU.add).then_inc(a_x1, 1)

            def root2(t, p, variances):
                ch = Chain(dve, c_rs, t + 1, 12)
                v, y, a = vv2[:, p, :], rs2[:, p, :], rtmp[:, :]
                ch(variances)
                ch(dve.tensor_scalar(y.bitcast(I32), v.bitcast(I32), 1, None, ALU.logical_shift_right))
                dve.tensor_scalar(vh[:, :], v, -0.5, None, ALU.mult)
                ch(dve.tensor_scalar(y.bitcast(I32), y.bitcast(I32), -1.0, float(0x5F3759DF), ALU.mult, ALU.add))
                for _ in range(3):
                    ch(dve.tensor_tensor(a, y, y, ALU.mult))
                    ch(dve.tensor_tensor(a, a, vh[:, :], ALU.mult))
                    ch(dve.scalar_tensor_tensor(y, a, 1.5, y, ALU.add, ALU.mult))
                ch.end()

            def period(t, r, k, lo, hi):
                p, o = r % 2, 1 - r % 2
                if lo <= 2 <= hi:
                    wait(dve, b_pv, t - 1)
                    ch = Chain(dve, c_x2, t - 2, 3)
                    ch(dve.reciprocal(ri2[:, p:p + 1], sm2[:, p:p + 1]))
                    dve.scalar_tensor_tensor(tile_of(t - 2), ps[:, 6, 0:DIM], ri2[:, p:p + 1], tile_of(t - 2),
                                             ALU.mult, ALU.add).then_inc(b_x2, 1)
                    wait_apart(dve, s_ready, b_x2, t - 1)
                    ch(dve.bn_stats(st3[:, p, :], tile_of(t - 2)), s_ready)
                    ch(dve.bn_aggr(mv3[:, p, :], st3[:, p, :]))
                    ch.end()
                    last = dve.tensor_scalar(vv2[:, p, 0:1], mv3[:, p, 1:2], EPS, None, ALU.add)
                if lo <= -1 <= hi:
                    ch = Chain(dve, c_ln2, t + 1, 2)
                    ch(dve.bn_stats(st2[:, o, :], tile_of(t + 1)), s_ready)
                    ch(dve.bn_aggr(mv2[:, o, :], st2[:, o, :]))
                    ch.end()
                    last = dve.tensor_scalar(vv2[:, p, 1:2], mv2[:, o, 1:2], EPS, None, ALU.add)
                if lo <= 2:
                    root2(t, p, last)
                if lo <= 2 <= hi:
                    rw = (r + 2) % STEP
                    wait(dve, b_scat[rw], 16 * TOPK * (k if r >= 2 else k - 1))
                    tok = rows[:, rw, ROW - 1:ROW].bitcast(I32)
                    dve.tensor_scalar(tok, tok, float(STEP * P), None, ALU.add)
                    dve.tensor_scalar(rows[:, rw, 0:DIM], tile_of(t - 2), mv3[:, p, 0:1], rs2[:, p, 0:1],
                                      ALU.subtract, ALU.mult).then_inc(b_x3n, 1)
                if lo <= -1 <= hi:
                    wait(dve, b_q2Tp, t)
                    dve.tensor_scalar(q2n[:, o, :], tile_of(t + 1), mv2[:, o, 0:1], rs2[:, p, 1:2],
                                      ALU.subtract, ALU.mult).then_inc(b_q2n, 1)
                if lo <= 3 <= hi:
                    rw = (r + 1) % STEP
                    wait(dve, b_lexp, t - 2)
                    ch = Chain(dve, c_rt, t - 3, 7)
                    ch(dve.reciprocal(gri[:, o:o + 1], gsum[:, o:o + 1]))
                    ch(dve.tensor_scalar(gt[:, o, :], gt[:, o, :], gri[:, o:o + 1], None, ALU.mult), s_ready)
                    ch(dve.max(top[:, o, :], gt[:, o, :]), s_ready)
                    ch(dve.match_replace(left[:, o, :], top[:, o, :], gt[:, o, :], -1.0))
                    ch(dve.tensor_scalar(mask[:, o, :], left[:, o, :], 0.0, None, ALU.is_lt))
                    wait(dve, b_rank, t - 3)
                    wait(dve, b_mask, t - 3)
                    dve.tensor_tensor(before[:, p, :], before[:, o, :], mask[:, o, :], ALU.add).then_inc(b_mask, 1)
                    ch(dve.tensor_reduce(tsum[:, o:o + 1], top[:, o, :], AX.X, ALU.add))
                    ch(dve.reciprocal(tsum[:, o:o + 1], tsum[:, o:o + 1]))
                    ch.end()
                    dve.tensor_scalar(rows[:, rw, DIM:DIM + EXPERTS], gt[:, o, :], tsum[:, o:o + 1], None, ALU.mult)
                if lo <= 0 <= hi:
                    ch = Chain(dve, c_mx, t, 1)
                    wait(dve, b_sc, 2 * t + 1)
                    flat = ps[:, 0:4, :].rearrange("p a b -> p (a b)")
                    dve.tensor_reduce(mx[:, p, 0:1], flat[:, 0:2 * BANK], AX.X, ALU.max)
                    wait(dve, b_sc, 2 * t + 2)
                    ch(dve.tensor_reduce(mx[:, p, 1:2], flat[:, 2 * BANK:KEYS], AX.X, ALU.max))
                    ch.end()
                    dve.tensor_reduce(nmx[:, p:p + 1], mx[:, p, :], AX.X, ALU.max, negate=True).then_inc(b_max, 1)
                if lo <= 3 <= hi:
                    rw = (r + 1) % STEP
                    wait(dve, b_rank, t - 2)
                    ch = Chain(dve, c_sl, t - 3, 3)
                    dve.tensor_scalar(over[:, :], ps[:, 7, 0:EXPERTS], float(CAP), FAR, ALU.is_ge, ALU.mult)
                    dve.tensor_tensor(slot[:, :], ps[:, 7, 0:EXPERTS], C[:, C_BASE:C_BASE + EXPERTS], ALU.add)\
                        .then_inc(b_rkd, 1)
                    wait(dve, b_rkd, t - 2)
                    ch(dve.tensor_tensor(slot[:, :], slot[:, :], over[:, :], ALU.add))
                    ch(dve.tensor_tensor(slot[:, :], slot[:, :], mask[:, o, :], ALU.mult), s_ready)
                    ch(dve.max(slot8[:, :], slot[:, :]))
                    ch.end()
                    dve.tensor_scalar(idx[:, rw, :], slot8[:, :], -1.0, None, ALU.add).then_inc(b_idx, 1)
                if lo <= 1 <= hi:
                    wait(dve, b_pv, t - 2)
                    wait(dve, b_pTp, 4 * (t - 1) + 3)
                    dve.tensor_copy(pT[:, o, 2 * BANK:3 * BANK], ps[:, 4, :]).then_inc(b_pTd, 1)
                    wait(dve, b_pTp, 4 * (t - 1) + 4)
                    dve.tensor_copy(pT[0:KLAST, o, 3 * BANK:3 * BANK + P], ps[0:KLAST, 5, 0:P]).then_inc(b_pTd, 1)
                if lo <= 2 <= hi:
                    wait(dve, b_lg, t - 1)
                    dve.tensor_reduce(nlm[:, p:p + 1], ps[:, 7, 0:EXPERTS], AX.X, ALU.max, negate=True)\
                        .then_inc(b_lmax, 1)

            periods(dve, period)

            def mul3(c, p):
                for j in range(FCH):
                    dve.wait_ge(d_sil, 3 * c + j + 1)
                    dve.wait_ge(d_up, 3 * c + j + 1)
                    if not (isinstance(c, int) and c < 2):
                        dve.wait_ge(d_y, c - 1)
                    dve.tensor_tensor(g3[:, p, j, :], sil3[:, j, :], ps[:, j, :], ALU.mult).then_inc(d_g, 1)

            def sum3(c, p):
                dve.wait_ge(d_y, c + 1)
                if not (isinstance(c, int) and c < 2):
                    dve.wait_ge(d_st[p], 16 * (c // 2))
                dve.tensor_tensor(o3[:, p, :, :].rearrange("p a c -> p (a c)"), ps[:, 6 + p, :],
                                  X[:, bass.ds(4 * c, 4), :].rearrange("p a c -> p (a c)"), ALU.add).then_inc(d_o, 1)

            mul3(0, 0)
            mul3(1, 1)
            sum3(0, 0)
            with dve.Fori(1, TOKENS // BANK // 2) as k:
                for p in range(2):
                    mul3(2 * k + p, p)
                    c = 2 * k + p - 1
                    dve.wait_ge(d_y, c + 1)
                    if p == 0:
                        dve.wait_ge(d_st[1], 16 * (k - 1))
                    else:
                        dve.wait_ge(d_st[0], 16 * k)
                    dve.tensor_tensor(o3[:, 1 - p, :, :].rearrange("p a c -> p (a c)"), ps[:, 7 - p, :],
                                      X[:, bass.ds(4 * c, 4), :].rearrange("p a c -> p (a c)"), ALU.add)\
                        .then_inc(d_o, 1)
            sum3(TOKENS // BANK - 1, 1)

            def step(e, i, k, lo, hi):
                p = i % 2
                if lo <= 0 <= hi:
                    if not (isinstance(e, int) and e < STEP):
                        dve.wait_ge(e_add[p], 32 * (2 * k + i // 2 - 1))
                    dve.wait_ge(r_in[i], 16 * (k + 1))
                    dve.tensor_copy(tok4[:, i, :], er[:, i, :, ROW - 1])
                    dve.tensor_copy(gate4[:, i, :], er[:, i, :, bass.ds(e + DIM, 1)].rearrange("p h a -> p (h a)"))\
                        .then_inc(e_row, 1)
                    dve.wait_ge(e_sil, e + 1)
                    dve.wait_ge(e_h, 2 * e + 2)
                    if not (isinstance(e, int) and e < 2):
                        dve.wait_ge(e_yTp, e - 1)
                    dve.tensor_tensor(g4[:, p, :], sil4[:, p, :], ps[:, 1 + p, 0:FCH * CAP], ALU.mult).then_inc(e_g, 1)
                if lo <= 2 <= hi:
                    i2 = (i + 2) % STEP
                    dve.wait_ge(e_yp, e - 1)
                    if not (isinstance(e, int) and e < STEP + 2):
                        dve.wait_ge(e_add[p], 32 * (2 * k + i // 2 - 2))
                    gate = gate4[:, i2, :].unsqueeze(2).to_broadcast([HALF, 2, DIM])
                    dve.tensor_tensor(yr[:, i2, :, :], ps[0:HALF, 6, 0:2 * DIM].rearrange("p (h c) -> p h c", h=2),
                                      gate, ALU.mult).then_inc(e_y, 1)

            steps(dve, step)


def periods(eng, period):
    period(-1, STEP - 1, -1, -1, -1)
    for t in range(STEP):
        period(t, t, 0, -1, t)
    with eng.Fori(1, TILES // STEP - 1) as k:
        for r in range(STEP):
            period(k * STEP + r, r, k, -1, 4)
    for t in range(TILES - STEP, TILES + 4):
        period(t, t % STEP, t // STEP, -1 if t < TILES - 1 else t - TILES + 1, 4)


def steps(eng, step):
    step(-1, STEP - 1, -1, -1, -1)
    for e in range(STEP):
        step(e, e, 0, -1, e)
    with eng.Fori(1, EXPERTS // STEP - 1) as k:
        for i in range(STEP):
            step(k * STEP + i, i, k, -1, 2)
    for e in range(EXPERTS - STEP, EXPERTS + 2):
        step(e, e % STEP, e // STEP, -1 if e < EXPERTS - 1 else e - EXPERTS + 1, 2)


def kernel(x, ctx_1024, L0_attn_Wq, L0_attn_bq, L0_attn_Wk, L0_attn_bk, L0_attn_Wv, L0_attn_bv, L0_attn_Wo,
           L0_attn_bo, L0_xattn_prefix_k, L0_xattn_prefix_v, L0_ffn_wg, L0_ffn_shared_w1, L0_ffn_shared_w2,
           L0_ffn_expert_w1, L0_ffn_expert_w2):
    import concourse.bacc as bacc
    from concourse.bass_utils import run_bass_kernel_spmd

    def lay(a):
        return np.ascontiguousarray(a)

    def packed(w1, w2):
        lead = w1.shape[:-2]
        a = np.swapaxes(w1, -1, -2)
        b = np.swapaxes(w2, -1, -2).reshape(*lead, FCH, P, DIM)
        b = np.moveaxis(b, -3, -2).reshape(*lead, P, FCH * DIM)
        return lay(np.concatenate([a, b], axis=-1))

    swap = np.arange(DIM) ^ 1
    x, ctx = np.asarray(x), np.asarray(ctx_1024)
    Wq, Wk, Wv, Wo = (np.asarray(w) for w in (L0_attn_Wq, L0_attn_Wk, L0_attn_Wv, L0_attn_Wo))
    bq, bk, bv, bo = (np.asarray(w) for w in (L0_attn_bq, L0_attn_bk, L0_attn_bv, L0_attn_bo))
    arrays = {
        "x": lay(x.reshape(TOKENS, DIM)),
        "ctxT": lay(ctx.transpose(0, 2, 1)),
        "ctxN": lay(ctx),
        "preT": lay(np.asarray(L0_xattn_prefix_k).T),
        "preV": lay(np.asarray(L0_xattn_prefix_v)),
        "wqkvo": lay(np.stack([Wq, Wq[:, swap], Wk, Wk[:, swap], Wv, Wo], axis=1)),
        "bcol": lay(np.stack([bq, bq[swap], bk, bk[swap], bv], axis=1)),
        "bo": lay(bo.reshape(1, DIM)),
        "wgT": lay(np.asarray(L0_ffn_wg).T),
        "sw": packed(np.asarray(L0_ffn_shared_w1), np.asarray(L0_ffn_shared_w2)),
        "ew": packed(np.asarray(L0_ffn_expert_w1), np.asarray(L0_ffn_expert_w2)),
        "cst": constants(),
    }
    nc = bacc.Bacc("TRN2", target_bir_lowering=False, num_devices=1)
    args = [nc.dram_tensor(n, a.shape, mybir.dt.from_np(a.dtype), kind="ExternalInput").ap() for n, a in arrays.items()]
    out = nc.dram_tensor("out", [TOKENS + SPARE, DIM], F32, kind="ExternalOutput").ap()
    decoder_layer(nc, *args, out)
    r = run_bass_kernel_spmd(nc, [arrays], core_ids=[0])
    return r.results[0]["out"][0:TOKENS].reshape(BATCHES, SEQ, DIM)
```

```python
from contextlib import ExitStack

import numpy as np

import concourse.bass as bass
from concourse import mybir

F32 = mybir.dt.float32
BF16 = mybir.dt.bfloat16
I32 = mybir.dt.int32
ALU = mybir.AluOpType
ACT = mybir.ActivationFunctionType
AX = mybir.AxisListType

P = 128
BATCHES, SEQ, DIM = 16, 256, 128
TOKENS = BATCHES * SEQ
TILES = TOKENS // P
CTX, PREFIX = 1601, 10
KEYS = CTX + PREFIX
KCH = -(-KEYS // P)
KLAST = KEYS - (KCH - 1) * P
CLAST = CTX - (KCH - 1) * P
EXPERTS, TOPK, CAP, FFN = 64, 8, 160, 384
FCH = FFN // P
SLOTS = EXPERTS * CAP
HALF = CAP // 2
SPARE = CAP
ZROWS = 76
ROW = DIM + EXPERTS + 1
EPS = 1e-5
GROUP = 4
STEP = 4
BANK = 512
CHOSEN = 16384
FLOAT_EPS = float(np.finfo(np.float32).eps)
FAR = 1.0e6
EW = 2 * FFN + FCH * DIM

C_ID, C_COS, C_SIN, C_MASK = 0, 128, 384, 640
C_TRI, C_BASE, C_END = 1024, 1152, 1216


def constants():
    c = np.zeros((P, C_END), np.float32)
    c[:, C_ID:C_ID + P] = np.eye(P)
    inv = (1.0 / np.float32(10000.0) ** (np.arange(0, DIM, 2, dtype=np.float32) / np.float32(DIM))).astype(np.float32)
    ang = np.repeat(np.arange(SEQ, dtype=np.float32)[:, None] * inv[None, :], 2, axis=-1)
    sign = np.where(np.arange(DIM) % 2 == 0, -1.0, 1.0).astype(np.float32)
    c[:, C_COS:C_COS + SEQ] = np.cos(ang).T
    c[:, C_SIN:C_SIN + SEQ] = np.sin(ang).T * sign[:, None]
    q = np.arange(P)[:, None]
    far = np.float32(-1e30)
    c[:, C_MASK:C_MASK + P] = np.where(np.arange(P)[None] <= q, 0, far)
    c[:, C_MASK + 2 * P:C_MASK + 3 * P] = c[:, C_MASK:C_MASK + P]
    c[:, C_TRI:C_TRI + P] = np.arange(P)[:, None] < np.arange(P)[None]
    c[:, C_BASE:C_BASE + EXPERTS] = np.arange(EXPERTS) * CAP + 1
    return c


def wait(eng, sem, value):
    if isinstance(value, int) and value <= 0:
        return
    eng.wait_ge(sem, value)


def wait_apart(eng, met, sem, value):
    if isinstance(value, int):
        return wait(eng, sem, value)
    value = eng.to_reg(value)
    eng.wait_ge(met, 1)
    eng.wait_ge(sem, value)


class Chain:

    def __init__(self, eng, sem, item, per):
        self.eng, self.sem, self.base, self.per, self.n = eng, sem, item * per, per, 0

    def __call__(self, instruction, met=None):
        instruction.then_inc(self.sem, 1)
        self.n += 1
        self.need(self.n, met)

    def mark(self, instruction):
        instruction.then_inc(self.sem, 1)
        self.n += 1
        return self.n

    def need(self, n, met=None):
        if met is not None:
            wait_apart(self.eng, met, self.sem, self.base + n)
        else:
            self.eng.wait_ge(self.sem, self.base + n)

    def end(self):
        assert self.n == self.per, (self.n, self.per)


def decoder_layer(nc, x, ctxT, ctxN, preT, preV, wqkvo, bcol, bo, wgT, sw, ew, cst, out):
    slots = nc.dram_tensor("slots", [SLOTS, ROW], F32, kind="Internal").ap()
    acc1 = nc.dram_tensor("acc1", [TOKENS + SPARE, DIM], F32, kind="Internal").ap()
    es = ExitStack()
    with es:
        def sb(name, shape, dt=F32):
            return es.enter_context(nc.sbuf_tensor(name, shape, dt))

        def sem(name):
            return es.enter_context(nc.semaphore(name))

        X = sb("X", [P, TILES, DIM])
        x3T = sb("x3T", [P, TOKENS])
        C = sb("C", [P, C_END])
        ident = C[:, C_ID:C_ID + P]
        W = sb("W", [P, 6, DIM])
        bias = sb("bias", [P, 5])
        bo_all = sb("bo_all", [P, DIM])
        WG = sb("WG", [P, EXPERTS])
        SW = sb("SW", [P, EW])
        mhalf = sb("mhalf", [P, 2 * GROUP])
        tri = sb("tri", [P, P], BF16)
        ones = sb("ones", [P, P], BF16)
        turn = sb("turn", [P, 1], BF16)
        chosen = sb("chosen", [P, P], BF16)
        st1 = sb("st1", [P, 2 * GROUP, 6])
        mv1 = sb("mv1", [P, 2 * GROUP, 2])
        rs1 = sb("rs1", [P, 2 * GROUP])
        vv1 = sb("vv1", [P, 2 * GROUP])
        xn = sb("xn", [P, 2 * GROUP, DIM])
        xnT = sb("xnT", [P, GROUP, SEQ])
        rc = sb("rc", [P, 2, 2 * SEQ])
        rsn = sb("rsn", [P, 2, 2 * SEQ])
        qk = sb("qk", [P, GROUP, 2 * SEQ])
        v1 = sb("v1", [P, GROUP, SEQ])
        pr = sb("pr", [P, GROUP, 3 * P])
        nm1 = sb("nm1", [P, GROUP, 2])
        sm1 = sb("sm1", [P, GROUP, 2])
        ri1 = sb("ri1", [P, GROUP, 2])
        prT = sb("prT", [P, GROUP, 3 * P])
        oT = sb("oT", [P, GROUP, SEQ])
        KT = sb("KT", [P, 2, KEYS])
        V = sb("V", [P, 2, KCH, DIM])
        st2 = sb("st2", [P, 2 * GROUP, 6])
        mv2 = sb("mv2", [P, 2 * GROUP, 2])
        vv2 = sb("vv2", [P, 2 * GROUP])
        ms2 = sb("ms2", [P, 2 * GROUP])
        rs2 = sb("rs2", [P, TILES])
        nm2 = sb("nm2", [P, TILES])
        q2n = sb("q2n", [P, 2, DIM])
        q2T = sb("q2T", [P, 2, P])
        mx = sb("mx", [P, 2, 4])
        nmx = sb("nmx", [P, 2])
        pe2 = sb("pe2", [P, 2, KEYS])
        sm2 = sb("sm2", [P, STEP])
        ri2 = sb("ri2", [P, 2])
        pT = sb("pT", [P, 2, KCH * P])
        st3 = sb("st3", [P, 2, 6])
        mv3 = sb("mv3", [P, 2, 2])
        vv3 = sb("vv3", [P, 2])
        vh3 = sb("vh3", [P, 2])
        ra3 = sb("ra3", [P, 2])
        rs3 = sb("rs3", [P, 2])
        rows = sb("rows", [P, STEP, ROW])
        x3s = sb("x3s", [P, 2, P])
        nlm = sb("nlm", [P, 2])
        gt = sb("gt", [P, 2, EXPERTS])
        gsum = sb("gsum", [P, 2])
        top = sb("top", [P, 2, TOPK])
        left = sb("left", [P, 2, EXPERTS])
        tsum = sb("tsum", [P, 2])
        mask = sb("mask", [P, 2, EXPERTS], BF16)
        before = sb("before", [P, 2, EXPERTS], BF16)
        over = sb("over", [P, EXPERTS])
        slot = sb("slot", [P, EXPERTS])
        slot8 = sb("slot8", [P, TOPK])
        idx = sb("idx", [P, STEP, TOPK], I32)
        blank = sb("blank", [HALF, 2, ROW])
        pe2f = pe2[:, :, :].rearrange("p a b -> p (a b)")
        pTf = pT[:, :, :].rearrange("p a b -> p (a b)")
        sil3 = pe2f[:, 0:FCH * BANK].rearrange("p (j c) -> p j c", j=FCH)
        o3 = pe2f[:, FCH * BANK:FCH * BANK + 2 * BANK].rearrange("p (a n c) -> p a n c", a=2, n=4)
        g3 = pTf[:, 0:2 * FCH * BANK].rearrange("p (a j c) -> p a j c", a=2, j=FCH)
        EWT = sb("EWT", [P, STEP, EW])
        er = sb("er", [HALF, STEP, 2, ROW])
        tok4 = sb("tok4", [HALF, STEP, 2])
        gate4 = sb("gate4", [HALF, STEP, 2])
        xeT = sb("xeT", [P, 2, CAP])
        sil4 = sb("sil4", [P, 2, FCH * CAP])
        g4 = sb("g4", [P, 2, FCH * CAP])
        yT = sb("yT", [P, 2, CAP])
        yr = sb("yr", [HALF, STEP, 2, DIM])

        ps = es.enter_context(nc.psum_tensor("ps", [P, 8, BANK], F32))

        s_const = sem("s_const")
        s_kvfix = sem("s_kvfix")
        s_blank = sem("s_blank")
        s_fill = sem("s_fill")
        s_ready = sem("s_ready")
        s_poolc = sem("s_poolc")
        a_x = sem("a_x")
        a_stats = sem("a_stats")
        a_rstd = sem("a_rstd")
        a_xn = sem("a_xn")
        a_xnTp = sem("a_xnTp")
        a_xnT = sem("a_xnT")
        a_qkv = sem("a_qkv")
        a_rope = sem("a_rope")
        a_qk = sem("a_qk")
        a_v = sem("a_v")
        a_sc = sem("a_sc")
        a_max = sem("a_max")
        a_exp = sem("a_exp")
        a_prob = sem("a_prob")
        a_prTp = sem("a_prTp")
        a_prT = sem("a_prT")
        a_oTp = sem("a_oTp")
        a_oT = sem("a_oT")
        a_outp = sem("a_outp")
        a_x1 = sem("a_x1")
        a_c1, a_c2, a_c3, a_c4 = sem("a_c1"), sem("a_c2"), sem("a_c3"), sem("a_c4")
        a_turn = sem("a_turn")
        a_stats2 = sem("a_stats2")
        a_neg2 = sem("a_neg2")
        a_rstd2 = sem("a_rstd2")
        a_norm2 = sem("a_norm2")
        k_in = [sem("k_in0"), sem("k_in1")]
        v_in = [sem("v_in0"), sem("v_in1")]
        b_q2n = sem("b_q2n")
        b_q2Tp = sem("b_q2Tp")
        b_q2T = sem("b_q2T")
        b_sc = sem("b_sc")
        b_max = sem("b_max")
        b_exp = sem("b_exp")
        b_pTp = sem("b_pTp")
        b_pTa = sem("b_pTa")
        b_pTb = sem("b_pTb")
        b_pTd = sem("b_pTd")
        b_pv = sem("b_pv")
        b_x2 = sem("b_x2")
        b_x3n = sem("b_x3n")
        b_x3Tp = sem("b_x3Tp")
        b_x3T = sem("b_x3T")
        b_lg = sem("b_lg")
        b_lmax = sem("b_lmax")
        b_lexp = sem("b_lexp")
        b_mask = sem("b_mask")
        b_rank = sem("b_rank")
        b_rkd = sem("b_rkd")
        b_idx = sem("b_idx")
        b_ri = sem("b_ri")
        b_wsum = sem("b_wsum")
        b_scat = [sem(f"b_scat{i}") for i in range(STEP)]
        c_x3, c_rt, c_sl, c_mx = (sem(n) for n in ("c_x3", "c_rt", "c_sl", "c_mx"))
        d_gate = sem("d_gate")
        d_up = sem("d_up")
        d_sil = sem("d_sil")
        d_g = sem("d_g")
        d_y = sem("d_y")
        d_o = sem("d_o")
        d_st = [sem("d_st0"), sem("d_st1")]
        w_in = [sem(f"w_in{i}") for i in range(STEP)]
        r_in = [sem(f"r_in{i}") for i in range(STEP)]
        e_xTp = sem("e_xTp")
        e_xT = sem("e_xT")
        e_row = sem("e_row")
        e_h = sem("e_h")
        e_sil = sem("e_sil")
        e_g = sem("e_g")
        e_yTp = sem("e_yTp")
        e_yT = sem("e_yT")
        e_yp = sem("e_yp")
        e_y = sem("e_y")
        e_add = [sem("e_add0"), sem("e_add1")]
        f_add = sem("f_add")

        def tile_of(t):
            return X[:, bass.ds(t, 1), :].rearrange("p a c -> p (a c)")

        block = es.enter_context(nc.Block())

        @block.sync
        def _(sp):
            half = TILES // 2
            xt = x.rearrange("(n p) c -> p n c", p=P)
            sp.dma_start(X[:, 0:8, :], xt[:, 0:8, :]).then_inc(s_const, 16)
            sp.dma_start(C[:, :], cst).then_inc(s_const, 16)
            sp.dma_start(W[:, :, :], wqkvo).then_inc(s_const, 16)
            sp.dma_start(bias[:, :], bcol).then_inc(s_const, 16)
            sp.dma_start(bo_all[:, :], bo.to_broadcast([P, DIM])).then_inc(s_const, 16)
            sp.dma_start(X[:, 8:TILES, :], xt[:, 8:TILES, :]).then_inc(s_const, 16)
            sp.dma_start(WG[:, :], wgT).then_inc(s_const, 16)
            sp.dma_start(SW[:, :], sw).then_inc(s_const, 16)
            for p in range(2):
                sp.dma_start(KT[:, p, CTX:KEYS], preT).then_inc(s_kvfix, 16)
                sp.dma_start(V[CLAST:KLAST, p, KCH - 1, :], preV).then_inc(s_kvfix, 16)

            def load_ctx(b, p, after):
                if after:
                    sp.wait_ge(b_sc, 4 * (b - 1))
                sp.dma_start(KT[:, p, 0:CTX], ctxT[b]).then_inc(k_in[p], 16)
                if after:
                    sp.wait_ge(b_pv, 2 * (b - 1))
                whole = (KCH - 1) * P
                src = ctxN[b]
                sp.dma_start(V[:, p, 0:KCH - 1, :], src[0:whole, :].rearrange("(n p) c -> p n c", p=P))\
                    .then_inc(v_in[p], 16)
                sp.dma_start(V[0:CLAST, p, KCH - 1, :], src[whole:CTX, :]).then_inc(v_in[p], 16)

            load_ctx(0, 0, False)
            load_ctx(1, 1, False)
            sp.wait_ge(s_blank, 1)
            for h in range(2):
                sp.dma_start(slots.rearrange("(n h p) c -> h p n c", h=2, p=HALF)[h],
                             blank[:, h, :].unsqueeze(1).to_broadcast([HALF, EXPERTS, ROW])).then_inc(s_fill, 16)
            rest = (TOKENS + SPARE) // ZROWS
            sp.dma_start(acc1.rearrange("(n p) c -> p n c", p=ZROWS),
                         blank[0:ZROWS, 0, 0:DIM].unsqueeze(1).to_broadcast([ZROWS, rest, DIM])).then_inc(s_fill, 16)
            sp.dma_start(out[TOKENS:TOKENS + SPARE, :].rearrange("(h p) c -> p h c", h=2), blank[:, :, 0:DIM])\
                .then_inc(s_fill, 16)
            with sp.Fori(1, BATCHES // 2) as k:
                for p in range(2):
                    load_ctx(2 * k + p, p, True)

            def load_expert(e, i, after):
                if after:
                    sp.wait_ge(e_yTp, e - STEP + 1)
                sp.dma_start(EWT[:, i, :], ew[e]).then_inc(w_in[i], 16)

            def load_rows(e, i):
                sp.dma_start(er[:, i, :, :], slots[bass.ds(e * CAP, CAP), :].rearrange("(h p) c -> p h c", h=2))\
                    .then_inc(r_in[i], 16)

            for i in range(STEP):
                load_expert(i, i, False)
            ov = out[0:TOKENS, :].rearrange("(n p) c -> p n c", p=P)
            with sp.Fori(0, TOKENS // BANK // 2) as k:
                for p in range(2):
                    sp.wait_ge(d_o, 2 * k + p + 1)
                    sp.dma_start(ov[:, bass.ds(8 * k + 4 * p, 4), :], o3[:, p, :, :]).then_inc(d_st[p], 16)
            for i in range(STEP):
                sp.wait_ge(b_scat[i], 16 * TOPK * TILES // STEP)
            for i in range(STEP):
                load_rows(i, i)
            with sp.Fori(1, EXPERTS // STEP) as k:
                for i in range(STEP):
                    load_expert(k * STEP + i, i, True)
                    sp.wait_ge(e_xTp, (k - 1) * STEP + i + 1)
                    sp.wait_ge(e_row, (k - 1) * STEP + i + 1)
                    load_rows(k * STEP + i, i)

        @block.gpsimd
        def _(pool):
            last_slot, last_row = pool.to_reg(SLOTS - 1), pool.to_reg(TOKENS + SPARE - 1)
            pool.memset(ones[:, :], 1.0)
            pool.memset(mhalf[:, :], -0.5).then_inc(a_norm2, 1)
            pool.memset(before[:, :, :], 0.0).then_inc(s_poolc, 1)
            pool.memset(blank[:, :, :], 0.0).then_inc(s_poolc, 1)
            pool.wait_ge(s_poolc, 2)
            pool.iota(blank[:, :, ROW - 1:ROW].bitcast(I32), pattern=[[HALF, 2], [0, 1]], base=TOKENS,
                      channel_multiplier=1).then_inc(s_blank, 1)
            for i in range(STEP):
                pool.iota(rows[:, i, ROW - 1:ROW].bitcast(I32), pattern=[[0, 1]], base=P * (i - STEP),
                          channel_multiplier=1).then_inc(s_poolc, 1)
            pool.wait_ge(s_const, 8 * 16)

            with pool.Fori(0, BATCHES // GROUP) as g:
                for j in range(GROUP):
                    b = g * GROUP + j
                    pool.wait_ge(a_stats, b + 1)
                    pool.tensor_tensor(rs1[:, 2 * j:2 * j + 2], vv1[:, 2 * j:2 * j + 2], mhalf[:, 0:2], ALU.pow)\
                        .then_inc(a_rstd, 1)
                for j in range(GROUP):
                    b = g * GROUP + j
                    pool.wait_ge(a_xn, b + 1)
                    xb = X[:, bass.ds(2 * b, 2), :]
                    pool.tensor_tensor(xb, xb, bo_all[:, :].unsqueeze(1).to_broadcast([P, 2, DIM]), ALU.add)\
                        .then_inc(a_x, 1)
                    pool.wait_ge(a_rope, b + 1)
                    pool.tensor_tensor(qk[:, j, :], rc[:, j % 2, :], rsn[:, j % 2, :], ALU.add).then_inc(a_qk, 1)
                wait_apart(pool, s_blank, a_stats2, GROUP * (g + 1))
                pool.tensor_scalar(ms2[:, :], mv2[:, :, 0], -1.0, None, ALU.mult).then_inc(a_neg2, 1)
                rs = rs2[:, bass.ds(2 * GROUP * g, 2 * GROUP)]
                pool.tensor_tensor(rs, vv2[:, :], mhalf[:, :], ALU.pow).then_inc(a_rstd2, 1)
                pool.wait_ge(a_neg2, g + 1)
                pool.wait_ge(a_rstd2, g + 1)
                pool.tensor_tensor(nm2[:, bass.ds(2 * GROUP * g, 2 * GROUP)], ms2[:, :], rs, ALU.mult)\
                    .then_inc(a_norm2, 1)

            def scatter(t, r, ks):
                wait_apart(pool, s_blank, b_idx, t + 1)
                for k in ks:
                    pool.indirect_dma_start(slots, bass.IndirectOffsetOnAxis(ap=idx[:, r, k:k + 1], axis=0),
                                            rows[:, r, :], None, bounds_check=last_slot, oob_is_err=False)\
                        .then_inc(b_scat[r], 16)

            def period(t, r, k, lo, hi):
                if lo <= 3 <= hi:
                    scatter(t - 3, (r + 1) % STEP, range(TOPK))

            pool.wait_ge(s_fill, 64)
            periods(pool, period)

            def add(e, i, k):
                if not (isinstance(e, int) and e < 2):
                    pool.wait_ge(e_add[i % 2], 32 * (2 * k + i // 2))
                wait_apart(pool, s_blank, e_y, e + 1)
                for h in range(2):
                    acc = out if i % 2 == 0 else acc1
                    pool.indirect_dma_start(
                        acc, bass.IndirectOffsetOnAxis(ap=tok4[:, i, h:h + 1].bitcast(I32), axis=0),
                        yr[:, i, h, :], None, bounds_check=last_row, oob_is_err=True,
                        compute_op=ALU.add).then_inc(e_add[i % 2], 16)

            for p in range(2):
                pool.wait_ge(d_st[p], 16 * (TOKENS // BANK // 2))
            for i in range(STEP):
                add(i, i, 0)
            with pool.Fori(1, EXPERTS // STEP) as k:
                for i in range(STEP):
                    add(k * STEP + i, i, k)
            for p in range(2):
                pool.wait_ge(e_add[p], 32 * (EXPERTS // 2))
            pool.dma_start(out[0:TOKENS, :].rearrange("(p r) c -> p (r c)", p=P),
                           acc1[0:TOKENS, :].rearrange("(p r) c -> p (r c)", p=P),
                           accum_op=ALU.add, max_dma_last_dim=4096).then_inc(f_add, 16)
            pool.wait_ge(f_add, 16)

        @block.tensor
        def _(pe):
            pe.wait_ge(s_const, 8 * 16)
            mm, tr = pe.matmul, pe.transpose
            with pe.Fori(0, BATCHES // GROUP) as g:
                for j in range(GROUP):
                    b = g * GROUP + j
                    pe.wait_ge(a_xn, b + 1)
                    if j < 2:
                        if j == 0:
                            pe.wait_ge(a_turn, g + 1)
                    else:
                        pe.wait_ge(a_xnT, b - 1)
                    tr(ps[:, j % 2, 0:P], xn[:, 2 * j, :], ident)
                    tr(ps[:, j % 2, P:2 * P], xn[:, 2 * j + 1, :], ident).then_inc(a_xnTp, 1)
                for j in range(GROUP):
                    b = g * GROUP + j
                    pe.wait_ge(a_xnT, b + 1)
                    if j >= 2:
                        pe.wait_ge(a_rope, b - 1)
                        pe.wait_ge(a_v, b - 1)
                    for w, (bank, col) in enumerate([(2, 0), (4, 0), (2, SEQ), (4, SEQ)]):
                        mm(ps[:, bank + j % 2, col:col + SEQ], W[:, w, :], xnT[:, j, :], start=True, stop=True)
                    for i in range(2):
                        last = mm(ps[:, 6 + j % 2, i * P:(i + 1) * P], xnT[:, j, i * P:(i + 1) * P], W[:, 4, :],
                                  start=True, stop=True)
                    last.then_inc(a_qkv, 1)
                for j in range(GROUP):
                    b = g * GROUP + j
                    pe.wait_ge(a_qk, b + 1)
                    if j == 0:
                        pe.wait_ge(a_rope, b + GROUP)
                    if j >= 2:
                        pe.wait_ge(a_max, b - 1)
                    mm(ps[:, 2 + j % 2, 0:P], qk[:, j, 0:P], qk[:, j, SEQ:SEQ + P], start=True, stop=True)
                    mm(ps[:, 2 + j % 2, P:3 * P], qk[:, j, P:2 * P], qk[:, j, SEQ:2 * SEQ], start=True,
                       stop=True).then_inc(a_sc, 1)
                for j in range(GROUP):
                    b = g * GROUP + j
                    pe.wait_ge(a_prob, b + 1)
                    if j >= 2:
                        pe.wait_ge(a_prT, b - 1)
                    for i in range(3):
                        last = tr(ps[:, 4 + j % 2, i * P:(i + 1) * P], pr[:, j, i * P:(i + 1) * P], ident)
                    last.then_inc(a_prTp, 1)
                for j in range(GROUP):
                    b = g * GROUP + j
                    pe.wait_ge(a_prT, b + 1)
                    if j == 0:
                        pe.wait_ge(a_v, b + GROUP)
                    if j >= 2:
                        pe.wait_ge(a_oT, b - 1)
                    o = ps[:, 6 + j % 2, :]
                    mm(o[:, 0:SEQ], v1[:, j, 0:P], prT[:, j, 0:SEQ], start=True, stop=False)
                    mm(o[:, P:SEQ], v1[:, j, P:SEQ], prT[:, j, SEQ:3 * P], start=False, stop=True).then_inc(a_oTp, 1)
                for j in range(GROUP):
                    b = g * GROUP + j
                    pe.wait_ge(a_oT, b + 1)
                    if j >= 2:
                        pe.wait_ge(a_x1, b - 1)
                    for i in range(2):
                        last = mm(ps[:, j % 2, i * P:(i + 1) * P], oT[:, j, i * P:(i + 1) * P], W[:, 5, :],
                                  start=True, stop=True)
                    last.then_inc(a_outp, 1)

            def period(t, r, k, lo, hi):
                p = r % 2
                o = 1 - p
                batch = (r // 2) % 2
                if lo <= 0 <= hi:
                    wait(pe, b_q2T, t + 1)
                    wait(pe, b_exp, t)
                    if p == 0:
                        pe.wait_ge(k_in[batch], 16 * (k + 1))
                    for i in range(4):
                        c0, c1 = i * BANK, min(KEYS, (i + 1) * BANK)
                        last = mm(ps[:, i, 0:c1 - c0], q2T[:, p, :], KT[:, batch, c0:c1], start=True, stop=True)
                        if i % 2:
                            last.then_inc(b_sc, 1)
                def transposed(gr):
                    wait(pe, b_exp, t)
                    if gr == 1:
                        wait(pe, b_pTd, 2 * (t - 1))
                    if gr == 2:
                        wait(pe, b_pTa, t)
                    if gr == 3:
                        wait(pe, b_pTb, t)
                    for n in range(4 * gr, min(KCH, 4 * gr + 4)):
                        w = P if n < KCH - 1 else KLAST
                        last = tr(ps[0:w, 4 + gr % 2, (n % 4) * P:(n % 4 + 1) * P], pe2[:, o, n * P:n * P + w], ident)
                    last.then_inc(b_pTp, 1)

                def values(n0, n1):
                    for n in range(n0, n1):
                        w = P if n < KCH - 1 else KLAST
                        last = mm(ps[:, 6, 0:DIM], pT[0:w, o, n * P:(n + 1) * P], V[0:w, vb, n, :],
                                  start=(n == 0), stop=(n == KCH - 1))
                    return last

                vb = (((r + STEP - 1) % STEP) // 2) % 2
                if lo <= 1 <= hi:
                    transposed(0)
                    transposed(1)
                if lo <= 3 <= hi:
                    wait(pe, b_mask, t - 2)
                    wait(pe, b_lexp, t - 2)
                    mm(ps[:, 7, 0:EXPERTS], tri[:, :], mask[:, o, :], start=True, stop=False)
                    mm(ps[:, 7, 0:EXPERTS], chosen[:, :], mask[:, o, :], start=False, stop=False)
                    mm(ps[:, 7, 0:EXPERTS], ones[:, :], before[:, o, :], start=False, stop=True).then_inc(b_rank, 1)
                if lo <= 1 <= hi:
                    transposed(2)
                    transposed(3)
                    wait(pe, b_x2, t - 1)
                    if o == 0:
                        pe.wait_ge(v_in[vb], 32 * (k + 1))
                    wait(pe, b_pTa, t)
                    wait(pe, b_pTb, t)
                    values(0, 8)
                if lo <= -1 <= hi:
                    wait(pe, b_q2n, t + 2)
                    if lo <= 1 <= hi:
                        wait(pe, b_pTd, 2 * t - 1)
                    tr(ps[:, 4, 0:P], q2n[:, o, :], ident).then_inc(b_q2Tp, 1)
                if lo <= 2 <= hi:
                    wait(pe, b_x3n, t - 1)
                    wait(pe, b_rkd, t - 2)
                    tr(ps[:, 7, 0:P], rows[:, (r + 2) % STEP, 0:DIM], ident).then_inc(b_x3Tp, 1)
                if lo <= 1 <= hi:
                    wait(pe, b_pTd, 2 * t)
                    values(8, KCH).then_inc(b_pv, 1)
                if lo <= 2 <= hi:
                    wait(pe, b_x3T, t - 1)
                    mm(ps[:, 7, 0:EXPERTS], x3s[:, p, :], WG[:, :], start=True, stop=True).then_inc(b_lg, 1)

            pe.wait_ge(a_x1, BATCHES)
            pe.wait_ge(s_kvfix, 64)
            pe.wait_ge(s_ready, 1)
            pe.wait_ge(s_poolc, 2)
            periods(pe, period)

            def up3(c, p):
                for j in range(FCH):
                    if not (isinstance(c, int) and c == 0):
                        pe.wait_ge(d_g, 3 * c - FCH + j + 1)
                    for bank, f, s in ((3 + j, FFN + j * P, d_gate), (j, j * P, d_up)):
                        mm(ps[:, bank, :], SW[:, f:f + P], x3T[:, bass.ds(c * BANK, BANK)],
                           start=True, stop=True).then_inc(s, 1)

            def down3(c, p):
                pe.wait_ge(d_g, 3 * c + 3)
                if not (isinstance(c, int) and c < 2):
                    pe.wait_ge(d_o, c - 1)
                for i in range(4):
                    for j in range(FCH):
                        last = mm(ps[:, 6 + p, i * P:(i + 1) * P], g3[:, p, j, i * P:(i + 1) * P],
                                  SW[:, 2 * FFN + j * DIM:2 * FFN + (j + 1) * DIM],
                                  start=(j == 0), stop=(j == FCH - 1))
                last.then_inc(d_y, 1)

            pe.wait_ge(b_x3T, TILES)
            pe.wait_ge(b_lexp, TILES)
            pe.wait_ge(b_rkd, TILES)
            up3(0, 0)
            up3(1, 1)
            down3(0, 0)
            with pe.Fori(1, TOKENS // BANK // 2) as k:
                for p in range(2):
                    up3(2 * k + p, p)
                    down3(2 * k + p - 1, 1 - p)
            down3(TOKENS // BANK - 1, 1)

            def step(e, i, k, lo, hi):
                p = i % 2
                if lo <= 0 <= hi:
                    pe.wait_ge(e_xT, e + 1)
                    pe.wait_ge(w_in[i], 16 * (k + 1))
                    if not (isinstance(e, int) and e < 2):
                        pe.wait_ge(e_g, e - 1)
                    for f0, bank in ((FFN, 3), (0, 1)):
                        for j in range(FCH):
                            last = mm(ps[:, bank + p, j * CAP:(j + 1) * CAP], EWT[:, i, f0 + j * P:f0 + (j + 1) * P],
                                      xeT[:, p, :], start=True, stop=True)
                        last.then_inc(e_h, 1)
                if lo <= 1 <= hi:
                    pe.wait_ge(e_g, e)
                    if not (isinstance(e, int) and e < 2):
                        pe.wait_ge(e_yT, e - 1)
                    w = EWT[:, (i - 1) % STEP, 2 * FFN:]
                    for j in range(FCH):
                        last = mm(ps[:, 5, 0:CAP], w[:, j * DIM:(j + 1) * DIM], g4[:, 1 - p, j * CAP:(j + 1) * CAP],
                                  start=(j == 0), stop=(j == FCH - 1))
                    last.then_inc(e_yTp, 1)
                if lo <= 2 <= hi:
                    pe.wait_ge(e_yT, e - 1)
                    if not (isinstance(e, int) and e < 3):
                        pe.wait_ge(e_y, e - 2)
                    for h in range(2):
                        last = tr(ps[0:HALF, 6, h * P:(h + 1) * P], yT[:, p, h * HALF:(h + 1) * HALF], ident)
                    last.then_inc(e_yp, 1)
                if lo <= -1 <= hi:
                    i1 = (i + 1) % STEP
                    pe.wait_ge(r_in[i1], 16 * (k + 1 + (i + 1) // STEP))
                    if not (isinstance(e, int) and e < 0):
                        pe.wait_ge(e_xT, e + 1)
                    for h in range(2):
                        last = tr(ps[:, 0, h * HALF:(h + 1) * HALF], er[:, i1, h, 0:DIM], ident[0:HALF, 0:HALF])
                    last.then_inc(e_xTp, 1)

            pe.wait_ge(d_o, TOKENS // BANK)
            steps(pe, step)

        @block.scalar
        def _(act):
            act.wait_ge(s_const, 8 * 16)
            with act.Fori(0, BATCHES // GROUP) as g:
                for j in range(GROUP):
                    b = g * GROUP + j
                    act.wait_ge(a_xnTp, b + 1)
                    act.activation(xnT[:, j, :], ps[:, j % 2, 0:SEQ], ACT.Copy).then_inc(a_xnT, 1)
                for j in range(GROUP):
                    b = g * GROUP + j
                    act.wait_ge(a_qkv, b + 1)
                    act.activation(v1[:, j, :], ps[:, 6 + j % 2, 0:SEQ], ACT.Copy).then_inc(a_v, 1)
                for j in range(GROUP):
                    b = g * GROUP + j
                    act.wait_ge(a_max, b + 1)
                    for i, (c0, c1) in enumerate(((0, P), (P, 3 * P))):
                        last = act.activation(pr[:, j, c0:c1], pr[:, j, c0:c1], ACT.Exp, bias=nm1[:, j, i:i + 1],
                                              accum_out=sm1[:, j, i:i + 1])
                    last.then_inc(a_exp, 1)
                for j in range(GROUP):
                    b = g * GROUP + j
                    act.wait_ge(a_prTp, b + 1)
                    act.activation(prT[:, j, :], ps[:, 4 + j % 2, 0:3 * P], ACT.Copy).then_inc(a_prT, 1)
                for j in range(GROUP):
                    b = g * GROUP + j
                    act.wait_ge(a_oTp, b + 1)
                    act.activation(oT[:, j, :], ps[:, 6 + j % 2, 0:SEQ], ACT.Identity, bias=bias[:, 4:5])\
                        .then_inc(a_oT, 1)

            def period(t, r, k, lo, hi):
                p, o = r % 2, 1 - r % 2
                if lo <= 3 <= hi:
                    wait(act, b_lmax, t - 2)
                    act.activation(gt[:, o, :], ps[:, 7, 0:EXPERTS], ACT.Exp, bias=nlm[:, o:o + 1],
                                   accum_out=gsum[:, o:o + 1]).then_inc(b_lexp, 1)
                if lo <= -1 <= hi:
                    wait(act, b_q2Tp, t)
                    act.activation(q2n[:, o, :], tile_of(t + 1), ACT.Identity, bias=nm2[:, bass.ds(t + 1, 1)],
                                   scale=rs2[:, bass.ds(t + 1, 1)]).then_inc(b_q2n, 1)
                if lo <= 1 <= hi:
                    for gr, s in ((0, b_pTa), (1, b_pTb)):
                        wait(act, b_pTp, 4 * (t - 1) + gr + 1)
                        wait(act, b_pv, t - 2)
                        act.activation(pT[:, o, gr * BANK:(gr + 1) * BANK], ps[:, 4 + gr, :], ACT.Copy).then_inc(s, 1)
                if lo <= 0 <= hi:
                    wait(act, b_max, t + 1)
                    wait(act, b_pTp, 4 * (t - 1))
                    act.activation(pe2[:, p, :], ps[:, 0:4, :].rearrange("p a b -> p (a b)")[:, 0:KEYS], ACT.Exp,
                                   bias=nmx[:, p:p + 1], accum_out=sm2[:, r:r + 1]).then_inc(b_exp, 1)
                if lo <= -1 <= hi:
                    wait(act, b_q2Tp, t + 2)
                    act.activation(q2T[:, o, :], ps[:, 4, 0:P], ACT.Copy).then_inc(b_q2T, 1)
                if lo <= 2 <= hi:
                    wait(act, b_x3Tp, t - 1)
                    act.activation(x3s[:, p, :], ps[:, 7, 0:P], ACT.Copy)
                    act.activation(x3T[:, bass.ds((t - 2) * P, P)], ps[:, 7, 0:P], ACT.Copy).then_inc(b_x3T, 1)

            act.wait_ge(a_norm2, BATCHES // GROUP + 1)
            periods(act, period)

            def silu3(c):
                for j in range(FCH):
                    act.wait_ge(d_gate, 3 * c + j + 1)
                    if not (isinstance(c, int) and c == 0):
                        act.wait_ge(d_g, 3 * c - FCH + j + 1)
                    act.activation(sil3[:, j, :], ps[:, 3 + j, :], ACT.Silu).then_inc(d_sil, 1)

            silu3(0)
            with act.Fori(1, TOKENS // BANK) as c:
                silu3(c)

            def step(e, i, k, lo, hi):
                p = i % 2
                if lo <= 0 <= hi:
                    act.wait_ge(e_h, 2 * e + 1)
                    act.activation(sil4[:, p, :], ps[:, 3 + p, 0:FCH * CAP], ACT.Silu).then_inc(e_sil, 1)
                if lo <= 1 <= hi:
                    act.wait_ge(e_yTp, e)
                    if not (isinstance(e, int) and e < 3):
                        act.wait_ge(e_yp, e - 2)
                    act.activation(yT[:, 1 - p, :], ps[:, 5, 0:CAP], ACT.Copy).then_inc(e_yT, 1)
                if lo <= -1 <= hi:
                    act.wait_ge(e_xTp, e + 2)
                    act.activation(xeT[:, 1 - p, :], ps[:, 0, 0:CAP], ACT.Copy).then_inc(e_xT, 1)

            steps(act, step)

        @block.vector
        def _(dve):
            dve.wait_ge(s_const, 8 * 16)
            dve.tensor_copy(tri[:, :], C[:, C_TRI:C_TRI + P])
            dve.tensor_scalar(chosen[:, :], ident, float(CHOSEN), None, ALU.mult).then_inc(s_ready, 1)
            dve.wait_ge(s_poolc, 2 + STEP)
            dve.tensor_copy(turn[:, :], ones[:, 0:1]).then_inc(a_turn, 1)
            with dve.Fori(0, BATCHES // GROUP) as g:
                for j in range(GROUP):
                    b = g * GROUP + j
                    ch = Chain(dve, a_c1, b, 2)
                    for i in range(2):
                        last = dve.bn_stats(st1[:, 2 * j + i, :], tile_of(2 * b + i))
                    ch(last, s_ready)
                    for i in range(2):
                        last = dve.bn_aggr(mv1[:, 2 * j + i, :], st1[:, 2 * j + i, :])
                    ch(last)
                    ch.end()
                    dve.tensor_scalar(vv1[:, 2 * j:2 * j + 2], mv1[:, 2 * j:2 * j + 2, 1], EPS, None, ALU.add)\
                        .then_inc(a_stats, 1)
                for j in range(GROUP):
                    b = g * GROUP + j
                    dve.wait_ge(a_rstd, b + 1)
                    for i in range(2):
                        n = 2 * j + i
                        last = dve.tensor_scalar(xn[:, n, :], tile_of(2 * b + i),
                                                 mv1[:, n, 0:1], rs1[:, n:n + 1], ALU.subtract, ALU.mult)
                    last.then_inc(a_xn, 1)
                for j in range(GROUP):
                    b = g * GROUP + j
                    dve.wait_ge(a_qkv, b + 1)
                    if j >= 2:
                        dve.wait_ge(a_qk, b - 1)
                    for w in range(2):
                        cols = slice(w * SEQ, (w + 1) * SEQ)
                        dve.scalar_tensor_tensor(rc[:, j % 2, cols], ps[:, 2 + j % 2, cols], bias[:, 2 * w:2 * w + 1],
                                                 C[:, C_COS:C_COS + SEQ], ALU.add, ALU.mult)
                        last = dve.scalar_tensor_tensor(rsn[:, j % 2, cols], ps[:, 4 + j % 2, cols],
                                                        bias[:, 2 * w + 1:2 * w + 2], C[:, C_SIN:C_SIN + SEQ],
                                                        ALU.add, ALU.mult)
                    last.then_inc(a_rope, 1)
                for j in range(GROUP):
                    b = g * GROUP + j
                    dve.wait_ge(a_sc, b + 1)
                    ch = Chain(dve, a_c2, b, 1)
                    ch(dve.scalar_tensor_tensor(pr[:, j, :], ps[:, 2 + j % 2, 0:3 * P], float(DIM) ** -0.5,
                                                C[:, C_MASK:C_MASK + 3 * P], ALU.mult, ALU.add))
                    ch.end()
                    dve.tensor_reduce(nm1[:, j, 0:1], pr[:, j, 0:P], AX.X, ALU.max, negate=True)
                    dve.tensor_reduce(nm1[:, j, 1:2], pr[:, j, P:3 * P], AX.X, ALU.max, negate=True).then_inc(a_max, 1)
                for j in range(GROUP):
                    b = g * GROUP + j
                    dve.wait_ge(a_exp, b + 1)
                    ch = Chain(dve, a_c3, b, 1)
                    ch(dve.reciprocal(ri1[:, j, :], sm1[:, j, :]))
                    ch.end()
                    dve.tensor_scalar(pr[:, j, 0:P], pr[:, j, 0:P], ri1[:, j, 0:1], None, ALU.mult)
                    dve.tensor_scalar(pr[:, j, P:3 * P], pr[:, j, P:3 * P], ri1[:, j, 1:2], None, ALU.mult)\
                        .then_inc(a_prob, 1)
                for j in range(GROUP):
                    b = g * GROUP + j
                    dve.wait_ge(a_outp, b + 1)
                    dve.wait_ge(a_x, b + 1)
                    xb = X[:, bass.ds(2 * b, 2), :].rearrange("p a c -> p (a c)")
                    dve.tensor_tensor(xb, ps[:, j % 2, 0:SEQ], xb, ALU.add).then_inc(a_x1, 1)
                    if j == 0:
                        wait_apart(dve, s_ready, a_norm2, g + 1)
                    wait_apart(dve, s_ready, a_x1, b + 1)
                    ch = Chain(dve, a_c4, b, 4)
                    for i in range(2):
                        n = ch.mark(dve.bn_stats(st2[:, 2 * j + i, :], X[:, bass.ds(2 * b + i, 1), :]
                                                 .rearrange("p a c -> p (a c)")))
                    for i in range(2):
                        ch.need(n - 1 + i, s_ready)
                        ch.mark(dve.bn_aggr(mv2[:, 2 * j + i, :], st2[:, 2 * j + i, :]))
                    ch.need(4)
                    ch.end()
                    dve.tensor_scalar(vv2[:, 2 * j:2 * j + 2], mv2[:, 2 * j:2 * j + 2, 1], EPS, None, ALU.add)\
                        .then_inc(a_stats2, 1)
                dve.tensor_copy(turn[:, :], ones[:, 0:1]).then_inc(a_turn, 1)

            def period(t, r, k, lo, hi):
                p, o = r % 2, 1 - r % 2
                now, last, prev, third = lo <= 0 <= hi, lo <= 1 <= hi, lo <= 2 <= hi, lo <= 3 <= hi
                x3, rt, sl, mc = Chain(dve, c_x3, t - 2, 12), Chain(dve, c_rt, t - 3, 5), \
                    Chain(dve, c_sl, t - 3, 2), Chain(dve, c_mx, t, 2)
                row2, row3 = (r + 2) % STEP, (r + 1) % STEP
                v, vh, a, y = (buf[:, p:p + 1] for buf in (vv3, vh3, ra3, rs3))

                def newton_a():
                    x3.mark(dve.scalar_tensor_tensor(a, y, vh, y, ALU.mult, ALU.mult))

                def newton_y():
                    x3.need(x3.n)
                    x3.mark(dve.scalar_tensor_tensor(y, a, 1.5, y, ALU.add, ALU.mult))

                if third:
                    wait(dve, b_lg, t - 2)
                    dve.tensor_reduce(nlm[:, o:o + 1], ps[:, 7, 0:EXPERTS], AX.X, ALU.max, negate=True)\
                        .then_inc(b_lmax, 1)
                if prev:
                    wait(dve, b_pv, t - 1)
                    dve.scalar_tensor_tensor(tile_of(t - 2), ps[:, 6, 0:DIM], ri2[:, p:p + 1], tile_of(t - 2),
                                             ALU.mult, ALU.add).then_inc(b_x2, 1)
                if last:
                    wait(dve, b_exp, t)
                    dve.reciprocal(ri2[:, o:o + 1], sm2[:, (r - 1) % STEP:(r - 1) % STEP + 1]).then_inc(b_ri, 1)
                if prev:
                    wait_apart(dve, s_ready, b_x2, t - 1)
                    x3(dve.bn_stats(st3[:, p, :], tile_of(t - 2)), s_ready)
                    n_aggr = x3.mark(dve.bn_aggr(mv3[:, p, :], st3[:, p, :]))
                if third:
                    wait_apart(dve, s_ready, b_lexp, t - 2)
                    n_top = rt.mark(dve.max(top[:, o, :], gt[:, o, :]))
                if prev:
                    x3.need(n_aggr)
                    n_v = x3.mark(dve.tensor_scalar(v, mv3[:, p, 1:2], EPS, None, ALU.add))
                if third:
                    rt.need(n_top, s_ready)
                    n_left = rt.mark(dve.match_replace(left[:, o, :], top[:, o, :], gt[:, o, :], -1.0))
                if prev:
                    x3.need(n_v)
                    n_y = x3.mark(dve.tensor_scalar(y.bitcast(I32), v.bitcast(I32), 1, None, ALU.logical_shift_right))
                    x3.mark(dve.tensor_scalar(vh, v, -0.5, None, ALU.mult))
                if third:
                    rt.need(n_left)
                    n_mask = rt.mark(dve.tensor_scalar(mask[:, o, :], left[:, o, :], 0.0, None, ALU.is_lt))
                if prev:
                    x3.need(n_y)
                    n_y = x3.mark(dve.tensor_scalar(y.bitcast(I32), y.bitcast(I32), -1.0, float(0x5F3759DF),
                                                    ALU.mult, ALU.add))
                if third:
                    rt.need(n_mask)
                    wait(dve, b_rank, t - 3)
                    wait(dve, b_mask, t - 3)
                    dve.tensor_tensor(before[:, p, :], before[:, o, :], mask[:, o, :], ALU.add).then_inc(b_mask, 1)
                    n_sum = rt.mark(dve.tensor_reduce(tsum[:, o:o + 1], top[:, o, :], AX.X, ALU.add))
                if prev:
                    x3.need(n_y)
                    newton_a()
                if third:
                    rt.need(n_sum)
                    n_sum = rt.mark(dve.scalar_tensor_tensor(tsum[:, o:o + 1], gsum[:, o:o + 1], FLOAT_EPS,
                                                             tsum[:, o:o + 1], ALU.mult, ALU.max))
                if now:
                    wait(dve, b_sc, 2 * t + 1)
                    flat = ps[:, 0:4, :].rearrange("p a b -> p (a b)")
                    mc.mark(dve.tensor_reduce(mx[:, p, 0:1], flat[:, 0:2 * BANK], AX.X, ALU.max))
                if prev:
                    newton_y()
                if third:
                    rt.need(n_sum)
                    dve.reciprocal(tsum[:, o:o + 1], tsum[:, o:o + 1]).then_inc(b_wsum, 1)
                if prev:
                    x3.need(x3.n)
                    newton_a()
                    wait(dve, b_scat[row2], 16 * TOPK * (k if r >= 2 else k - 1))
                    tok = rows[:, row2, ROW - 1:ROW].bitcast(I32)
                    dve.tensor_scalar(tok, tok, float(STEP * P), None, ALU.add)
                if third:
                    wait(dve, b_wsum, t - 2)
                    dve.tensor_scalar(rows[:, row3, DIM:DIM + EXPERTS], gt[:, o, :], tsum[:, o:o + 1], None, ALU.mult)
                if prev:
                    newton_y()
                if now:
                    wait(dve, b_sc, 2 * t + 2)
                    n_max = mc.mark(dve.tensor_reduce(mx[:, p, 1:2], flat[:, 2 * BANK:KEYS], AX.X, ALU.max))
                if prev:
                    x3.need(x3.n)
                    newton_a()
                if now:
                    mc.need(n_max)
                    dve.tensor_reduce(nmx[:, p:p + 1], mx[:, p, 0:2], AX.X, ALU.max, negate=True).then_inc(b_max, 1)
                if prev:
                    newton_y()
                if third:
                    wait(dve, b_rank, t - 2)
                    dve.tensor_scalar(over[:, :], ps[:, 7, 0:EXPERTS], float(CHOSEN + CAP), FAR, ALU.is_ge, ALU.mult)
                    dve.tensor_tensor(slot[:, :], ps[:, 7, 0:EXPERTS], C[:, C_BASE:C_BASE + EXPERTS], ALU.add)\
                        .then_inc(b_rkd, 1)
                if prev:
                    x3.need(x3.n)
                    dve.tensor_scalar(rows[:, row2, 0:DIM], tile_of(t - 2), mv3[:, p, 0:1], y,
                                      ALU.subtract, ALU.mult).then_inc(b_x3n, 1)
                if third:
                    wait(dve, b_rkd, t - 2)
                    n_slot = sl.mark(dve.tensor_tensor(slot[:, :], slot[:, :], over[:, :], ALU.add))
                if last:
                    wait(dve, b_pv, t - 2)
                    wait(dve, b_pTp, 4 * (t - 1) + 3)
                    dve.tensor_copy(pT[:, o, 2 * BANK:3 * BANK], ps[:, 4, :]).then_inc(b_pTd, 1)
                if third:
                    sl.need(n_slot, s_ready)
                    n_slot = sl.mark(dve.max(slot8[:, :], slot[:, :]))
                if last:
                    wait(dve, b_pTp, 4 * (t - 1) + 4)
                    dve.tensor_copy(pT[0:KLAST, o, 3 * BANK:3 * BANK + P], ps[0:KLAST, 5, 0:P]).then_inc(b_pTd, 1)
                if third:
                    sl.need(n_slot)
                    dve.tensor_scalar(idx[:, row3, :], slot8[:, :], -1.0 - CHOSEN, None, ALU.add).then_inc(b_idx, 1)

            periods(dve, period)

            def mul3(c, p):
                for j in range(FCH):
                    dve.wait_ge(d_sil, 3 * c + j + 1)
                    dve.wait_ge(d_up, 3 * c + j + 1)
                    if not (isinstance(c, int) and c < 2):
                        dve.wait_ge(d_y, c - 1)
                    dve.tensor_tensor(g3[:, p, j, :], sil3[:, j, :], ps[:, j, :], ALU.mult).then_inc(d_g, 1)

            def sum3(c, p):
                dve.wait_ge(d_y, c + 1)
                if not (isinstance(c, int) and c < 2):
                    dve.wait_ge(d_st[p], 16 * (c // 2))
                dve.tensor_tensor(o3[:, p, :, :].rearrange("p a c -> p (a c)"), ps[:, 6 + p, :],
                                  X[:, bass.ds(4 * c, 4), :].rearrange("p a c -> p (a c)"), ALU.add).then_inc(d_o, 1)

            mul3(0, 0)
            mul3(1, 1)
            sum3(0, 0)
            def two3(k):
                for p in range(2):
                    mul3(2 * k + p, p)
                    c = 2 * k + p - 1
                    dve.wait_ge(d_y, c + 1)
                    wait(dve, d_st[1 - p], 16 * (k - 1 + p))
                    dve.tensor_tensor(o3[:, 1 - p, :, :].rearrange("p a c -> p (a c)"), ps[:, 7 - p, :],
                                      X[:, bass.ds(4 * c, 4), :].rearrange("p a c -> p (a c)"), ALU.add)\
                        .then_inc(d_o, 1)

            two3(1)
            with dve.Fori(2, TOKENS // BANK // 2) as k:
                two3(k)
            sum3(TOKENS // BANK - 1, 1)

            def step(e, i, k, lo, hi):
                p = i % 2
                if lo <= 0 <= hi:
                    dve.wait_ge(e_sil, e + 1)
                    dve.wait_ge(e_h, 2 * e + 2)
                    if not (isinstance(e, int) and e < 2):
                        dve.wait_ge(e_yTp, e - 1)
                    dve.tensor_tensor(g4[:, p, :], sil4[:, p, :], ps[:, 1 + p, 0:FCH * CAP], ALU.mult).then_inc(e_g, 1)
                if lo <= 2 <= hi:
                    i2 = (i + 2) % STEP
                    dve.wait_ge(e_yp, e - 1)
                    dve.wait_ge(e_row, e - 1)
                    gate = gate4[:, i2, :].unsqueeze(2).to_broadcast([HALF, 2, DIM])
                    dve.tensor_tensor(yr[:, i2, :, :], ps[0:HALF, 6, 0:2 * DIM].rearrange("p (h c) -> p h c", h=2),
                                      gate, ALU.mult).then_inc(e_y, 1)
                if lo <= 0 <= hi:
                    if not (isinstance(e, int) and e < STEP):
                        dve.wait_ge(e_add[p], 32 * (2 * k + i // 2 - 1))
                    dve.wait_ge(r_in[i], 16 * (k + 1))
                    dve.tensor_copy(tok4[:, i, :], er[:, i, :, ROW - 1])
                    dve.tensor_copy(gate4[:, i, :], er[:, i, :, bass.ds(e + DIM, 1)].rearrange("p h a -> p (h a)"))\
                        .then_inc(e_row, 1)

            steps(dve, step)


def periods(eng, period):
    period(-1, STEP - 1, -1, -1, -1)
    for t in range(STEP):
        period(t, t, 0, -1, t)
    with eng.Fori(1, TILES // STEP - 1) as k:
        for r in range(STEP):
            period(k * STEP + r, r, k, -1, 4)
    for t in range(TILES - STEP, TILES + 4):
        period(t, t % STEP, t // STEP, -1 if t < TILES - 1 else t - TILES + 1, 4)


def steps(eng, step):
    step(-1, STEP - 1, -1, -1, -1)
    for e in range(STEP):
        step(e, e, 0, -1, e)
    with eng.Fori(1, EXPERTS // STEP - 1) as k:
        for i in range(STEP):
            step(k * STEP + i, i, k, -1, 2)
    for e in range(EXPERTS - STEP, EXPERTS + 2):
        step(e, e % STEP, e // STEP, -1 if e < EXPERTS - 1 else e - EXPERTS + 1, 2)


def kernel(x, ctx_1024, L0_attn_Wq, L0_attn_bq, L0_attn_Wk, L0_attn_bk, L0_attn_Wv, L0_attn_bv, L0_attn_Wo,
           L0_attn_bo, L0_xattn_prefix_k, L0_xattn_prefix_v, L0_ffn_wg, L0_ffn_shared_w1, L0_ffn_shared_w2,
           L0_ffn_expert_w1, L0_ffn_expert_w2):
    import concourse.bacc as bacc
    from concourse.bass_utils import run_bass_kernel_spmd

    def lay(a):
        return np.ascontiguousarray(a)

    def packed(w1, w2):
        lead = w1.shape[:-2]
        a = np.swapaxes(w1, -1, -2)
        b = np.swapaxes(w2, -1, -2).reshape(*lead, FCH, P, DIM)
        b = np.moveaxis(b, -3, -2).reshape(*lead, P, FCH * DIM)
        return lay(np.concatenate([a, b], axis=-1))

    swap = np.arange(DIM) ^ 1
    x, ctx = np.asarray(x), np.asarray(ctx_1024)
    Wq, Wk, Wv, Wo = (np.asarray(w) for w in (L0_attn_Wq, L0_attn_Wk, L0_attn_Wv, L0_attn_Wo))
    bq, bk, bv, bo = (np.asarray(w) for w in (L0_attn_bq, L0_attn_bk, L0_attn_bv, L0_attn_bo))
    arrays = {
        "x": lay(x.reshape(TOKENS, DIM)),
        "ctxT": lay(ctx.transpose(0, 2, 1)),
        "ctxN": lay(ctx),
        "preT": lay(np.asarray(L0_xattn_prefix_k).T),
        "preV": lay(np.asarray(L0_xattn_prefix_v)),
        "wqkvo": lay(np.stack([Wq, Wq[:, swap], Wk, Wk[:, swap], Wv, Wo], axis=1)),
        "bcol": lay(np.stack([bq, bq[swap], bk, bk[swap], bv], axis=1)),
        "bo": lay(bo.reshape(1, DIM)),
        "wgT": lay(np.asarray(L0_ffn_wg).T),
        "sw": packed(np.asarray(L0_ffn_shared_w1), np.asarray(L0_ffn_shared_w2)),
        "ew": packed(np.asarray(L0_ffn_expert_w1), np.asarray(L0_ffn_expert_w2)),
        "cst": constants(),
    }
    nc = bacc.Bacc("TRN2", target_bir_lowering=False, num_devices=1)
    args = [nc.dram_tensor(n, a.shape, mybir.dt.from_np(a.dtype), kind="ExternalInput").ap() for n, a in arrays.items()]
    out = nc.dram_tensor("out", [TOKENS + SPARE, DIM], F32, kind="ExternalOutput").ap()
    decoder_layer(nc, *args, out)
    r = run_bass_kernel_spmd(nc, [arrays], core_ids=[0])
    return r.results[0]["out"][0:TOKENS].reshape(BATCHES, SEQ, DIM)
```

```python
from contextlib import ExitStack

import numpy as np

import concourse.bass as bass
from concourse import mybir

F32 = mybir.dt.float32
BF16 = mybir.dt.bfloat16
I32 = mybir.dt.int32
ALU = mybir.AluOpType
ACT = mybir.ActivationFunctionType
AX = mybir.AxisListType

P = 128
BATCHES, SEQ, DIM = 16, 256, 128
TOKENS = BATCHES * SEQ
TILES = TOKENS // P
CTX, PREFIX = 1601, 10
KEYS = CTX + PREFIX
KCH = -(-KEYS // P)
KLAST = KEYS - (KCH - 1) * P
CLAST = CTX - (KCH - 1) * P
EXPERTS, TOPK, CAP, FFN = 64, 8, 160, 384
FCH = FFN // P
SLOTS = EXPERTS * CAP
HALF = CAP // 2
SPARE = CAP
ZROWS = 76
ROW = DIM + EXPERTS + 1
EPS = 1e-5
STEP = 4
RING = 8
BANK = 512
CHOSEN = 16384
FLOAT_EPS = float(np.finfo(np.float32).eps)
FAR = 1.0e6
EW = 2 * FFN + FCH * DIM

C_ID, C_MASK, C_TRI, C_BASE = 0, P, 2 * P, 3 * P
C_COS = C_BASE + EXPERTS
C_SIN = C_COS + 2 * SEQ
C_END = C_SIN + 2 * SEQ


def constants():
    c = np.zeros((P, C_END), np.float32)
    c[:, C_ID:C_ID + P] = np.eye(P)
    inv = (1.0 / np.float32(10000.0) ** (np.arange(0, DIM, 2, dtype=np.float32) / np.float32(DIM))).astype(np.float32)
    ang = np.repeat(np.arange(SEQ, dtype=np.float32)[:, None] * inv[None, :], 2, axis=-1)
    sign = np.where(np.arange(DIM) % 2 == 0, -1.0, 1.0).astype(np.float32)
    for w, scale in enumerate((np.float32(DIM) ** -0.5, 1.0)):
        c[:, C_COS + w * SEQ:C_COS + (w + 1) * SEQ] = np.cos(ang).T * scale
        c[:, C_SIN + w * SEQ:C_SIN + (w + 1) * SEQ] = np.sin(ang).T * sign[:, None] * scale
    c[:, C_MASK:C_MASK + P] = np.where(np.arange(P)[None] <= np.arange(P)[:, None], 0, np.float32(-1e30))
    c[:, C_TRI:C_TRI + P] = np.arange(P)[:, None] < np.arange(P)[None]
    c[:, C_BASE:C_BASE + EXPERTS] = np.arange(EXPERTS) * CAP + 1
    return c


def wait(eng, sem, value):
    if isinstance(value, int) and value <= 0:
        return
    eng.wait_ge(sem, value)


def wait_apart(eng, met, sem, value):
    if isinstance(value, int):
        return wait(eng, sem, value)
    value = eng.to_reg(value)
    eng.wait_ge(met, 1)
    eng.wait_ge(sem, value)


class Chain:

    def __init__(self, eng, sem, item, per):
        self.eng, self.sem, self.base, self.per, self.n = eng, sem, item * per, per, 0

    def __call__(self, instruction, met=None):
        instruction.then_inc(self.sem, 1)
        self.n += 1
        self.need(self.n, met)

    def mark(self, instruction):
        instruction.then_inc(self.sem, 1)
        self.n += 1
        return self.n

    def need(self, n, met=None):
        if met is not None:
            wait_apart(self.eng, met, self.sem, self.base + n)
        else:
            self.eng.wait_ge(self.sem, self.base + n)


def decoder_layer(nc, x, ctxT, ctxN, preT, preV, wqkvo, bcol, bo, wgT, sw, ew, cst, out):
    slots = nc.dram_tensor("slots", [SLOTS, ROW], F32, kind="Internal").ap()
    acc1 = nc.dram_tensor("acc1", [TOKENS + SPARE, DIM], F32, kind="Internal").ap()
    es = ExitStack()
    with es:
        def sb(name, shape, dt=F32):
            return es.enter_context(nc.sbuf_tensor(name, shape, dt))

        def sem(name):
            return es.enter_context(nc.semaphore(name))

        X = sb("X", [P, TILES, DIM])
        x3T = sb("x3T", [P, TOKENS])
        C = sb("C", [P, C_END])
        ident = C[:, C_ID:C_ID + P]
        W = sb("W", [P, 6, DIM])
        bias = sb("bias", [P, 5])
        bo_all = sb("bo_all", [P, DIM])
        WG = sb("WG", [P, EXPERTS])
        SW = sb("SW", [P, EW])
        mhalf = sb("mhalf", [P, 2 * STEP])
        tri = sb("tri", [P, P], BF16)
        ones = sb("ones", [P, P], BF16)
        chosen = sb("chosen", [P, P], BF16)
        maskb = sb("maskb", [P, P], BF16)
        identb = sb("identb", [P, P], BF16)
        st1 = sb("st1", [P, 4, 6])
        mv1 = sb("mv1", [P, 4, 2])
        rs1 = sb("rs1", [P, 4])
        vv1 = sb("vv1", [P, 4])
        ng1 = sb("ng1", [P, 4])
        mr1 = sb("mr1", [P, 4])
        bv_all = sb("bv_all", [P, P])
        xn = sb("xn", [P, 4, DIM])
        xnT = sb("xnT", [P, 2, SEQ])
        rc = sb("rc", [P, 2, 2 * SEQ])
        rsn = sb("rsn", [P, 2, 2 * SEQ])
        qk = sb("qk", [P, 2, 2 * SEQ])
        v1 = sb("v1", [P, STEP, SEQ])
        pr = sb("pr", [P, 2, 3 * P])
        nm1 = sb("nm1", [P, 2, 2])
        sm1 = sb("sm1", [P, STEP, 2])
        ri1 = sb("ri1", [P, STEP, 2])
        prT = sb("prT", [P, 2, 3 * P])
        oT = sb("oT", [P, 2, SEQ])
        KT = sb("KT", [P, 2, KEYS])
        V = sb("V", [P, 2, KCH, DIM])
        st2 = sb("st2", [P, 2 * STEP, 6])
        mv2 = sb("mv2", [P, 2 * STEP, 2])
        vv2 = sb("vv2", [P, 2 * STEP])
        ms2 = sb("ms2", [P, 2 * STEP])
        rs2 = sb("rs2", [P, TILES])
        nm2 = sb("nm2", [P, TILES])
        q2n = sb("q2n", [P, 2, DIM])
        q2T = sb("q2T", [P, 2, P])
        mx = sb("mx", [P, 2, 4])
        nmx = sb("nmx", [P, 2])
        pe2 = sb("pe2", [P, 2, KEYS])
        sm2 = sb("sm2", [P, 4, 2])
        all2 = sb("all2", [P, 2])
        ri2 = sb("ri2", [P, 2])
        pT = sb("pT", [P, 2, KCH * P])
        st3 = sb("st3", [P, 2, 6])
        mv3 = sb("mv3", [P, 2, 2])
        vv3 = sb("vv3", [P, 2])
        vh3 = sb("vh3", [P, 2])
        ra3 = sb("ra3", [P, 2])
        rs3 = sb("rs3", [P, 2])
        rows = sb("rows", [P, RING, ROW])
        tok0 = sb("tok0", [P, RING], I32)
        x3s = sb("x3s", [P, 2, P])
        nlm = sb("nlm", [P, 2])
        gt = sb("gt", [P, 2, EXPERTS])
        gsum = sb("gsum", [P, 2])
        top = sb("top", [P, 2, TOPK])
        left = sb("left", [P, 2, EXPERTS])
        tsum = sb("tsum", [P, 2])
        mask = sb("mask", [P, 2, EXPERTS], BF16)
        before = sb("before", [P, 2, EXPERTS], BF16)
        over = sb("over", [P, EXPERTS])
        slot = sb("slot", [P, EXPERTS])
        slot8 = sb("slot8", [P, TOPK])
        idx = sb("idx", [P, RING, TOPK], I32)
        blank = sb("blank", [HALF, 2, ROW])
        pe2f = pe2[:, :, :].rearrange("p a b -> p (a b)")
        pTf = pT[:, :, :].rearrange("p a b -> p (a b)")
        sil3 = pe2f[:, 0:FCH * BANK].rearrange("p (j c) -> p j c", j=FCH)
        o3 = pe2f[:, FCH * BANK:FCH * BANK + 2 * BANK].rearrange("p (a n c) -> p a n c", a=2, n=4)
        g3 = pTf[:, 0:2 * FCH * BANK].rearrange("p (a j c) -> p a j c", a=2, j=FCH)
        EWT = sb("EWT", [P, STEP, EW])
        er = sb("er", [HALF, STEP, 2, ROW])
        tok4 = sb("tok4", [HALF, STEP, 2])
        gate4 = sb("gate4", [HALF, STEP, 2])
        xeT = sb("xeT", [P, 2, CAP])
        sil4 = sb("sil4", [P, 2, FCH * CAP])
        g4 = sb("g4", [P, 2, FCH * CAP])
        yT = sb("yT", [P, 2, CAP])
        yr = sb("yr", [HALF, STEP, 2, DIM])

        ps = es.enter_context(nc.psum_tensor("ps", [P, 8, BANK], F32))

        s_x0 = sem("s_x0")
        s_x1 = sem("s_x1")
        s_x2 = sem("s_x2")
        s_attn = sem("s_attn")
        s_rot = sem("s_rot")
        s_ffn = sem("s_ffn")
        s_bvw = sem("s_bvw")
        s_kvfix = sem("s_kvfix")
        s_blank = sem("s_blank")
        s_tok0 = sem("s_tok0")
        s_fill = sem("s_fill")
        s_ready = sem("s_ready")
        s_poolc = sem("s_poolc")
        a_x = sem("a_x")
        a_stats = sem("a_stats")
        a_pow = sem("a_pow")
        a_rstd = sem("a_rstd")
        a_xn = sem("a_xn")
        a_xnTp = sem("a_xnTp")
        a_xnT = sem("a_xnT")
        a_qkp = sem("a_qkp")
        a_vp = sem("a_vp")
        a_rope = sem("a_rope")
        a_qk = sem("a_qk")
        a_v = sem("a_v")
        a_sc = sem("a_sc")
        a_max = sem("a_max")
        a_exp = sem("a_exp")
        a_ri = sem("a_ri")
        a_prTp = sem("a_prTp")
        a_prT = sem("a_prT")
        a_oTp = sem("a_oTp")
        a_oT = sem("a_oT")
        a_outp = sem("a_outp")
        a_x1 = sem("a_x1")
        a_c1, a_c2 = sem("a_c1"), sem("a_c2")
        a_stats2 = sem("a_stats2")
        a_neg2 = sem("a_neg2")
        a_rstd2 = sem("a_rstd2")
        a_norm2 = sem("a_norm2")
        k_in = [sem("k_in0"), sem("k_in1")]
        v_in = [sem("v_in0"), sem("v_in1")]
        b_q2n = sem("b_q2n")
        b_q2Tp = sem("b_q2Tp")
        b_q2T = sem("b_q2T")
        b_sc = sem("b_sc")
        b_max = sem("b_max")
        b_exp = sem("b_exp")
        b_sum = sem("b_sum")
        b_pTp = sem("b_pTp")
        b_pTa = sem("b_pTa")
        b_pTb = sem("b_pTb")
        b_pTc = sem("b_pTc")
        b_pTd = sem("b_pTd")
        b_pv = sem("b_pv")
        b_x2 = sem("b_x2")
        b_x3n = sem("b_x3n")
        b_x3Tp = sem("b_x3Tp")
        b_x3T = sem("b_x3T")
        b_lg = sem("b_lg")
        b_lmax = sem("b_lmax")
        b_lexp = sem("b_lexp")
        b_mask = sem("b_mask")
        b_rank = sem("b_rank")
        b_rkd = sem("b_rkd")
        b_idx = sem("b_idx")
        b_ri = sem("b_ri")
        b_wsum = sem("b_wsum")
        b_scat = [sem(f"b_scat{i}") for i in range(RING)]
        c_x3, c_rt, c_sl, c_mx = (sem(n) for n in ("c_x3", "c_rt", "c_sl", "c_mx"))
        d_gate = sem("d_gate")
        d_up = sem("d_up")
        d_sil = sem("d_sil")
        d_g = sem("d_g")
        d_y = sem("d_y")
        d_o = sem("d_o")
        d_st = [sem("d_st0"), sem("d_st1")]
        w_in = [sem(f"w_in{i}") for i in range(STEP)]
        r_in = [sem(f"r_in{i}") for i in range(STEP)]
        e_xTp = sem("e_xTp")
        e_xT = sem("e_xT")
        e_row = sem("e_row")
        e_h = sem("e_h")
        e_sil = sem("e_sil")
        e_g = sem("e_g")
        e_yTp = sem("e_yTp")
        e_yT = sem("e_yT")
        e_yp = sem("e_yp")
        e_y = sem("e_y")
        e_add = [sem("e_add0"), sem("e_add1")]
        f_add = sem("f_add")

        def tile_of(t):
            return X[:, bass.ds(t, 1), :].rearrange("p a c -> p (a c)")

        block = es.enter_context(nc.Block())

        @block.sync
        def _(sp):
            xt = x.rearrange("(n p) c -> p n c", p=P)
            first, second = 4, 12
            sp.dma_start(X[:, 0:first, :], xt[:, 0:first, :]).then_inc(s_x0, 16)
            sp.dma_start(C[:, 0:C_COS], cst[:, 0:C_COS]).then_inc(s_attn, 16)
            sp.dma_start(W[:, :, :], wqkvo).then_inc(s_attn, 16)
            sp.dma_start(bias[:, :], bcol).then_inc(s_attn, 16)
            sp.dma_start(bo_all[:, :], bo.to_broadcast([P, DIM])).then_inc(s_attn, 16)
            sp.dma_start(C[:, C_COS:C_END], cst[:, C_COS:C_END]).then_inc(s_rot, 16)
            sp.dma_start(X[:, first:second, :], xt[:, first:second, :]).then_inc(s_x1, 16)
            sp.dma_start(X[:, second:TILES, :], xt[:, second:TILES, :]).then_inc(s_x2, 16)
            sp.dma_start(WG[:, :], wgT).then_inc(s_ffn, 16)
            sp.dma_start(SW[:, :], sw).then_inc(s_ffn, 16)
            for p in range(2):
                sp.dma_start(KT[:, p, CTX:KEYS], preT).then_inc(s_kvfix, 16)
                sp.dma_start(V[CLAST:KLAST, p, KCH - 1, :], preV).then_inc(s_kvfix, 16)

            def load_ctx(b, p, after):
                if after:
                    sp.wait_ge(b_sc, 4 * (b - 1))
                sp.dma_start(KT[:, p, 0:CTX], ctxT[b]).then_inc(k_in[p], 16)
                if after:
                    sp.wait_ge(b_pv, 2 * (b - 1))
                whole = (KCH - 1) * P
                src = ctxN[b]
                sp.dma_start(V[:, p, 0:KCH - 1, :], src[0:whole, :].rearrange("(n p) c -> p n c", p=P))\
                    .then_inc(v_in[p], 16)
                sp.dma_start(V[0:CLAST, p, KCH - 1, :], src[whole:CTX, :]).then_inc(v_in[p], 16)

            load_ctx(0, 0, False)
            load_ctx(1, 1, False)
            sp.wait_ge(s_blank, 1)
            for h in range(2):
                sp.dma_start(slots.rearrange("(n h p) c -> h p n c", h=2, p=HALF)[h],
                             blank[:, h, :].unsqueeze(1).to_broadcast([HALF, EXPERTS, ROW])).then_inc(s_fill, 16)
            rest = (TOKENS + SPARE) // ZROWS
            sp.dma_start(acc1.rearrange("(n p) c -> p n c", p=ZROWS),
                         blank[0:ZROWS, 0, 0:DIM].unsqueeze(1).to_broadcast([ZROWS, rest, DIM])).then_inc(s_fill, 16)
            sp.dma_start(out[TOKENS:TOKENS + SPARE, :].rearrange("(h p) c -> p h c", h=2), blank[:, :, 0:DIM])\
                .then_inc(s_fill, 16)
            with sp.Fori(1, BATCHES // 2) as k:
                for p in range(2):
                    load_ctx(2 * k + p, p, True)

            def load_expert(e, i, after):
                if after:
                    sp.wait_ge(e_yTp, e - STEP + 1)
                sp.dma_start(EWT[:, i, :], ew[e]).then_inc(w_in[i], 16)

            def load_rows(e, i):
                sp.dma_start(er[:, i, :, :], slots[bass.ds(e * CAP, CAP), :].rearrange("(h p) c -> p h c", h=2))\
                    .then_inc(r_in[i], 16)

            for i in range(STEP):
                load_expert(i, i, False)
            ov = out[0:TOKENS, :].rearrange("(n p) c -> p n c", p=P)

            def store(c, p):
                sp.wait_ge(d_o, c + 1)
                sp.dma_start(ov[:, bass.ds(4 * c, 4), :], o3[:, p, :, :]).then_inc(d_st[p], 16)

            chunks = TOKENS // BANK
            with sp.Fori(0, chunks // 2 - 1) as k:
                for p in range(2):
                    store(2 * k + p, p)
            for i in range(RING):
                sp.wait_ge(b_scat[i], 16 * (TOPK * TILES // RING + 1))
            for i in range(STEP):
                load_rows(i, i)
            for p in range(2):
                store(chunks - 2 + p, p)
            with sp.Fori(1, EXPERTS // STEP) as k:
                for i in range(STEP):
                    load_expert(k * STEP + i, i, True)
                    sp.wait_ge(e_xTp, (k - 1) * STEP + i + 1)
                    sp.wait_ge(e_row, (k - 1) * STEP + i + 1)
                    load_rows(k * STEP + i, i)

        @block.gpsimd
        def _(pool):
            last_slot, last_row = pool.to_reg(SLOTS - 1), pool.to_reg(TOKENS + SPARE - 1)
            pool.memset(ones[:, :], 1.0)
            pool.memset(mhalf[:, :], -0.5).then_inc(a_norm2, 1)
            pool.memset(before[:, :, :], 0.0).then_inc(s_poolc, 1)
            pool.memset(blank[:, :, :], 0.0).then_inc(s_poolc, 1)
            pool.wait_ge(s_poolc, 2)
            pool.iota(blank[:, :, ROW - 1:ROW].bitcast(I32), pattern=[[HALF, 2], [0, 1]], base=TOKENS,
                      channel_multiplier=1).then_inc(s_blank, 1)
            def period(b, r, k, lo, hi):
                if lo <= -1 <= hi:
                    if isinstance(b, int) and b == -1:
                        pool.wait_ge(s_bvw, 3)
                    pool.wait_ge(a_xn, b + 2)
                    xb = X[:, bass.ds(2 * (b + 1), 2), :]
                    pool.tensor_tensor(xb, xb, bo_all[:, :].unsqueeze(1).to_broadcast([P, 2, DIM]), ALU.add)\
                        .then_inc(a_x, 1)
                if lo <= 0 <= hi:
                    pool.wait_ge(a_rope, 2 * b + 2)
                    wait(pool, a_sc, b - 1)
                    pool.tensor_tensor(qk[:, r % 2, :], rc[:, r % 2, :], rsn[:, r % 2, :], ALU.add).then_inc(a_qk, 1)
                if lo <= -2:
                    n = 2 * (r % 2)
                    pool.wait_ge(a_stats, b + 3)
                    pool.tensor_tensor(rs1[:, n:n + 2], vv1[:, n:n + 2], mhalf[:, 0:2], ALU.pow).then_inc(a_pow, 1)
                    pool.wait_ge(a_pow, b + 3)
                    pool.tensor_tensor(mr1[:, n:n + 2], ng1[:, n:n + 2], rs1[:, n:n + 2], ALU.mult).then_inc(a_rstd, 1)
                if r == STEP - 1 and lo <= 4 <= hi:
                    wait_apart(pool, s_blank, a_stats2, b - 3)
                    pool.tensor_scalar(ms2[:, :], mv2[:, :, 0], -1.0, None, ALU.mult).then_inc(a_neg2, 1)
                    rs = rs2[:, bass.ds(2 * (b - 7), 2 * STEP)]
                    pool.tensor_tensor(rs, vv2[:, :], mhalf[:, :], ALU.pow).then_inc(a_rstd2, 1)
                    pool.wait_ge(a_neg2, k)
                    pool.wait_ge(a_rstd2, k)
                    pool.tensor_tensor(nm2[:, bass.ds(2 * (b - 7), 2 * STEP)], ms2[:, :], rs, ALU.mult)\
                        .then_inc(a_norm2, 1)

            periods(pool, period, BATCHES, 2, 4)

            pool.iota(tok0[:, :], pattern=[[P, RING]], base=-P * RING, channel_multiplier=1).then_inc(s_tok0, 1)
            pool.wait_ge(s_tok0, 1)
            for i in range(RING):
                pool.dma_start(rows[:, i, ROW - 1:ROW].bitcast(I32), tok0[:, i:i + 1]).then_inc(b_scat[i], 16)

            def scatter(t, r, ks):
                wait_apart(pool, s_blank, b_idx, t + 1)
                for k in ks:
                    pool.indirect_dma_start(slots, bass.IndirectOffsetOnAxis(ap=idx[:, r, k:k + 1], axis=0),
                                            rows[:, r, :], None, bounds_check=last_slot, oob_is_err=False)\
                        .then_inc(b_scat[r], 16)

            def period(t, r, floor, lo, hi):
                if lo <= 4 <= hi:
                    scatter(t - 4, (r - 4) % RING, range(TOPK))

            pool.wait_ge(s_fill, 64)
            tiles(pool, period)

            def add(e, i, k):
                if not (isinstance(e, int) and e < 2):
                    pool.wait_ge(e_add[i % 2], 32 * (2 * k + i // 2))
                wait_apart(pool, s_blank, e_y, e + 1)
                for h in range(2):
                    acc = out if i % 2 == 0 else acc1
                    pool.indirect_dma_start(
                        acc, bass.IndirectOffsetOnAxis(ap=tok4[:, i, h:h + 1].bitcast(I32), axis=0),
                        yr[:, i, h, :], None, bounds_check=last_row, oob_is_err=True,
                        compute_op=ALU.add).then_inc(e_add[i % 2], 16)

            for p in range(2):
                pool.wait_ge(d_st[p], 16 * (TOKENS // BANK // 2))
            for i in range(STEP):
                add(i, i, 0)
            with pool.Fori(1, EXPERTS // STEP) as k:
                for i in range(STEP):
                    add(k * STEP + i, i, k)
            for p in range(2):
                pool.wait_ge(e_add[p], 32 * (EXPERTS // 2))
            pool.dma_start(out[0:TOKENS, :].rearrange("(p r) c -> p (r c)", p=P),
                           acc1[0:TOKENS, :].rearrange("(p r) c -> p (r c)", p=P),
                           accum_op=ALU.add, max_dma_last_dim=4096).then_inc(f_add, 16)
            pool.wait_ge(f_add, 16)

        @block.tensor
        def _(pe):
            pe.wait_ge(s_attn, 4 * 16)
            mm, tr = pe.matmul, pe.transpose
            pe.wait_ge(s_bvw, 1)
            mm(ps[:, 6, 0:DIM], bv_all[:, :], W[:, 5, :], start=True, stop=True).then_inc(s_bvw, 1)
            pe.wait_ge(s_ready, 1)

            def attend(b, r, k, lo, hi):
                p, o = r % 2, 1 - r % 2
                if isinstance(b, int) and b == 0:
                    pe.wait_ge(s_bvw, 3)
                if lo <= 0 <= hi:
                    pe.wait_ge(a_xnT, b + 1)
                    for w in range(2):
                        wait(pe, a_rope, 2 * b + w - 1)
                        for i in range(2):
                            last = mm(ps[:, w, i * SEQ:(i + 1) * SEQ], W[:, 2 * w + i, :], xnT[:, p, :],
                                      start=True, stop=True)
                        last.then_inc(a_qkp, 1)
                    wait(pe, a_v, b)
                    for i in range(2):
                        last = mm(ps[:, 2, i * P:(i + 1) * P], xnT[:, p, i * P:(i + 1) * P], W[:, 4, :],
                                  start=True, stop=True)
                    last.then_inc(a_vp, 1)
                if lo <= -1 <= hi:
                    pe.wait_ge(a_xn, b + 2)
                    wait(pe, a_xnT, b + 1)
                    for i in range(2):
                        last = tr(ps[:, 7, i * P:(i + 1) * P], xn[:, 2 * o + i, :], ident)
                    last.then_inc(a_xnTp, 1)
                if lo <= 4 <= hi:
                    pe.wait_ge(a_oT, b - 3)
                    if isinstance(b, int):
                        wait(pe, a_x1, b - 4)
                    else:
                        pe.wait_ge(a_stats, b + 2)
                    for i in range(2):
                        last = mm(ps[:, 6, i * P:(i + 1) * P], oT[:, p, i * P:(i + 1) * P], W[:, 5, :],
                                  start=True, stop=True)
                    last.then_inc(a_outp, 1)
                if lo <= 1 <= hi:
                    pe.wait_ge(a_qk, b)
                    wait(pe, a_exp, b - 1)
                    for q0, c0, width in ((0, 0, P), (P, P, SEQ)):
                        mm(ps[:, 3, c0:c0 + width], qk[:, o, q0:q0 + P], qk[:, o, SEQ:SEQ + width],
                           start=True, stop=False)
                        last = mm(ps[:, 3, c0 + q0:c0 + q0 + P], identb[:, :], maskb[:, :], start=False, stop=True)
                    last.then_inc(a_sc, 1)
                if lo <= 2 <= hi:
                    pe.wait_ge(a_exp, b - 1)
                    wait(pe, a_prT, b - 2)
                    for i in range(3):
                        last = tr(ps[:, 4, i * P:(i + 1) * P], pr[:, p, i * P:(i + 1) * P], ident)
                    last.then_inc(a_prTp, 1)
                if lo <= 3 <= hi:
                    pe.wait_ge(a_prT, b - 2)
                    pe.wait_ge(a_v, b - 2)
                    wait(pe, a_oT, b - 3)
                    v = v1[:, (r + 1) % STEP, :]
                    mm(ps[:, 5, 0:SEQ], v[:, 0:P], prT[:, o, 0:SEQ], start=True, stop=False)
                    mm(ps[:, 5, P:SEQ], v[:, P:SEQ], prT[:, o, SEQ:3 * P], start=False, stop=True).then_inc(a_oTp, 1)

            periods(pe, attend, BATCHES, 2, 4, end=BATCHES + 2)

            def up3(c, j):
                if not (isinstance(c, int) and c == 0):
                    pe.wait_ge(d_g, 3 * c - FCH + j + 1)
                for bank, f, s in ((3 + j, FFN + j * P, d_gate), (j, j * P, d_up)):
                    mm(ps[:, bank, :], SW[:, f:f + P], x3T[:, bass.ds(c * BANK, BANK)],
                       start=True, stop=True).then_inc(s, 1)

            def period(t, r, floor, lo, hi):
                if isinstance(t, int) and t > TILES:
                    up3(0, t - TILES - 1)
                p, o = r % 2, 1 - r % 2
                batch = (r // 2) % 2
                before_batch = ((r - 1) // 2) % 2

                def scores(half):
                    wait(pe, b_exp, 2 * t - 1 + half)
                    for i in range(2 * half, 2 * half + 2):
                        c0, c1 = i * BANK, min(KEYS, (i + 1) * BANK)
                        last = mm(ps[:, i, 0:c1 - c0], q2T[:, p, :], KT[:, batch, c0:c1], start=True, stop=True)
                    last.then_inc(b_sc, 1)

                def transposed(gr):
                    wait(pe, b_exp, 2 * t - 1 + gr // 2)
                    if gr == 0 and lo <= -1:
                        wait(pe, b_q2T, t + 2)
                    if gr == 1:
                        wait(pe, b_pTd, t - 1)
                    if gr == 2:
                        wait(pe, b_pTa, t)
                    if gr == 3:
                        wait(pe, b_pTb, t)
                    for n in range(4 * gr, min(KCH, 4 * gr + 4)):
                        w = P if n < KCH - 1 else KLAST
                        last = tr(ps[0:w, 4 + gr % 2, (n % 4) * P:(n % 4 + 1) * P], pe2[:, o, n * P:n * P + w], ident)
                    last.then_inc(b_pTp, 1)

                def values(n0, n1):
                    for n in range(n0, n1):
                        w = P if n < KCH - 1 else KLAST
                        last = mm(ps[:, 6, 0:DIM], pT[0:w, o, n * P:(n + 1) * P], V[0:w, before_batch, n, :],
                                  start=(n == 0), stop=(n == KCH - 1))
                    return last

                if lo <= -1 <= hi:
                    wait(pe, b_q2n, t + 2)
                    tr(ps[:, 4, 0:P], q2n[:, o, :], ident).then_inc(b_q2Tp, 1)
                if lo <= 4 <= hi:
                    wait(pe, b_mask, t - 3)
                    wait(pe, b_lexp, t - 3)
                    mm(ps[:, 7, 0:EXPERTS], tri[:, :], mask[:, p, :], start=True, stop=False)
                    mm(ps[:, 7, 0:EXPERTS], chosen[:, :], mask[:, p, :], start=False, stop=False)
                    mm(ps[:, 7, 0:EXPERTS], ones[:, :], before[:, p, :], start=False, stop=True).then_inc(b_rank, 1)
                if lo <= 0 <= hi:
                    wait(pe, b_q2T, t + 1)
                    if p == 0:
                        pe.wait_ge(k_in[batch], 16 * (floor(0, 4) + 1))
                    scores(0)
                if lo <= 3 <= hi:
                    wait(pe, b_x3n, t - 2)
                    wait(pe, b_rkd, t - 3)
                    tr(ps[:, 7, 0:P], rows[:, (r - 3) % RING, 0:DIM], ident).then_inc(b_x3Tp, 1)
                if lo <= 1 <= hi:
                    transposed(0)
                    transposed(1)
                if lo <= 3 <= hi:
                    wait(pe, b_x3T, t - 2)
                    mm(ps[:, 7, 0:EXPERTS], x3s[:, o, :], WG[:, :], start=True, stop=True).then_inc(b_lg, 1)
                if lo <= 0 <= hi:
                    scores(1)
                if lo <= 1 <= hi:
                    transposed(2)
                    transposed(3)
                    if isinstance(t, int) and t == 1:
                        pe.wait_ge(a_x1, BATCHES)
                    wait(pe, b_x2, t - 1)
                    if o == 0:
                        pe.wait_ge(v_in[before_batch], 32 * (floor(1, 4) + 1))
                    wait(pe, b_pTa, t)
                    wait(pe, b_pTb, t)
                    values(0, 8)
                if lo <= 1 <= hi:
                    wait(pe, b_pTc, t)
                    wait(pe, b_pTd, t)
                    values(8, KCH).then_inc(b_pv, 1)

            for used in (a_v, a_exp, a_prT):
                pe.wait_ge(used, BATCHES)
            pe.wait_ge(a_rope, 2 * BATCHES)
            pe.wait_ge(s_kvfix, 64)
            pe.wait_ge(s_ffn, 2 * 16)
            pe.wait_ge(s_poolc, 2)
            pe.wait_ge(s_ready, 2)
            crossing(attend, period)
            tiles(pe, period, first=1)

            def down3(c, p):
                pe.wait_ge(d_g, 3 * c + 3)
                if not (isinstance(c, int) and c < 2):
                    pe.wait_ge(d_o, c - 1)
                for i in range(4):
                    for j in range(FCH):
                        last = mm(ps[:, 6 + p, i * P:(i + 1) * P], g3[:, p, j, i * P:(i + 1) * P],
                                  SW[:, 2 * FFN + j * DIM:2 * FFN + (j + 1) * DIM],
                                  start=(j == 0), stop=(j == FCH - 1))
                last.then_inc(d_y, 1)

            def step(e, i, k, lo, hi):
                p = i % 2
                if lo <= 0 <= hi:
                    pe.wait_ge(e_xT, e + 1)
                    pe.wait_ge(w_in[i], 16 * (k + 1))
                    if not (isinstance(e, int) and e < 2):
                        pe.wait_ge(e_g, e - 1)
                    for f0, bank in ((FFN, 3), (0, 1)):
                        for j in range(FCH):
                            last = mm(ps[:, bank + p, j * CAP:(j + 1) * CAP], EWT[:, i, f0 + j * P:f0 + (j + 1) * P],
                                      xeT[:, p, :], start=True, stop=True)
                        last.then_inc(e_h, 1)
                if lo <= -1 <= hi:
                    i1 = (i + 1) % STEP
                    pe.wait_ge(r_in[i1], 16 * (k + 1 + (i + 1) // STEP))
                    if not (isinstance(e, int) and e < 0):
                        pe.wait_ge(e_xT, e + 1)
                    for h in range(2):
                        last = tr(ps[:, 0, h * HALF:(h + 1) * HALF], er[:, i1, h, 0:DIM], ident[0:HALF, 0:HALF])
                    last.then_inc(e_xTp, 1)
                if lo <= 1 <= hi:
                    pe.wait_ge(e_g, e)
                    if not (isinstance(e, int) and e < 2):
                        pe.wait_ge(e_yT, e - 1)
                    w = EWT[:, (i - 1) % STEP, 2 * FFN:]
                    for j in range(FCH):
                        last = mm(ps[:, 5, 0:CAP], w[:, j * DIM:(j + 1) * DIM], g4[:, 1 - p, j * CAP:(j + 1) * CAP],
                                  start=(j == 0), stop=(j == FCH - 1))
                    last.then_inc(e_yTp, 1)
                if isinstance(e, int) and e == 2:
                    pe.wait_ge(d_o, TOKENS // BANK)
                if lo <= 2 <= hi:
                    pe.wait_ge(e_yT, e - 1)
                    if not (isinstance(e, int) and e < 3):
                        pe.wait_ge(e_y, e - 2)
                    for h in range(2):
                        last = tr(ps[0:HALF, 6, h * P:(h + 1) * P], yT[:, p, h * HALF:(h + 1) * HALF], ident)
                    last.then_inc(e_yp, 1)

            def ups(c):
                for j in range(FCH):
                    up3(c, j)

            def two3(k):
                for p in range(2):
                    ups(2 * k + p)
                    down3(2 * k + p - 1, 1 - p)

            ups(1)
            down3(0, 0)
            pe.wait_ge(b_x3T, TILES)
            pe.wait_ge(b_rkd, TILES)
            two3(1)
            with pe.Fori(2, TOKENS // BANK // 2) as k:
                two3(k)
            pe.wait_ge(d_g, FCH * (TOKENS // BANK - 1) + 1)
            step(-1, STEP - 1, -1, -1, -1)
            down3(TOKENS // BANK - 1, 1)
            periods(pe, step, EXPERTS, 1, 2, first=0)

        @block.scalar
        def _(act):
            def attend(b, r, k, lo, hi):
                p, o = r % 2, 1 - r % 2
                if lo <= -1 <= hi:
                    act.wait_ge(a_rstd, b + 2)
                    wait(act, a_xnTp, b)
                    for i in range(2):
                        n = 2 * o + i
                        last = act.activation(xn[:, n, :], tile_of(2 * (b + 1) + i), ACT.Identity,
                                              bias=mr1[:, n:n + 1], scale=rs1[:, n:n + 1])
                    last.then_inc(a_xn, 1)
                if lo <= 0 <= hi:
                    act.wait_ge(a_vp, b + 1)
                    act.activation(v1[:, r, :], ps[:, 2, 0:SEQ], ACT.Copy).then_inc(a_v, 1)
                if lo <= -1 <= hi:
                    act.wait_ge(a_xnTp, b + 2)
                    act.activation(xnT[:, o, :], ps[:, 7, 0:SEQ], ACT.Copy).then_inc(a_xnT, 1)
                if lo <= 2 <= hi:
                    act.wait_ge(a_prTp, b - 1)
                    act.activation(prT[:, p, :], ps[:, 4, 0:3 * P], ACT.Copy).then_inc(a_prT, 1)
                if lo <= 1 <= hi:
                    act.wait_ge(a_max, b)
                    for i, (c0, c1) in enumerate(((0, P), (P, 3 * P))):
                        last = act.activation(pr[:, o, c0:c1], ps[:, 3, c0:c1], ACT.Exp, bias=nm1[:, o, i:i + 1],
                                              accum_out=sm1[:, (r - 1) % STEP, i:i + 1])
                    last.then_inc(a_exp, 1)
                if lo <= 3 <= hi:
                    act.wait_ge(a_oTp, b - 2)
                    act.activation(oT[:, o, :], ps[:, 5, 0:SEQ], ACT.Copy).then_inc(a_oT, 1)

            periods(act, attend, BATCHES, 2, 4, end=BATCHES + 2)

            def period(t, r, floor, lo, hi):
                p, o = r % 2, 1 - r % 2
                if isinstance(t, int) and t in (-2, 3):
                    act.wait_ge(a_norm2, 2 if t < 0 else BATCHES // STEP + 1)
                if lo <= -1 <= hi:
                    wait(act, b_q2Tp, t + 2)
                    act.activation(q2T[:, o, :], ps[:, 4, 0:P], ACT.Copy).then_inc(b_q2T, 1)
                if lo <= 3 <= hi:
                    wait(act, b_x3Tp, t - 2)
                    act.activation(x3s[:, o, :], ps[:, 7, 0:P], ACT.Copy)
                    act.activation(x3T[:, bass.ds((t - 3) * P, P)], ps[:, 7, 0:P], ACT.Copy).then_inc(b_x3T, 1)
                if lo <= -2:
                    wait(act, b_q2Tp, t + 1)
                    act.activation(q2n[:, p, :], tile_of(t + 2), ACT.Identity, bias=nm2[:, bass.ds(t + 2, 1)],
                                   scale=rs2[:, bass.ds(t + 2, 1)]).then_inc(b_q2n, 1)

                def taken(gr, s):
                    wait(act, b_pTp, 4 * (t - 1) + gr + 1)
                    wait(act, b_pv, t - 2)
                    keys, rows_ = (BANK, P) if gr < 3 else (P, KLAST)
                    act.activation(pT[0:rows_, o, gr * BANK:gr * BANK + keys], ps[0:rows_, 4 + gr % 2, 0:keys],
                                   ACT.Copy).then_inc(s, 1)

                if lo <= 1 <= hi:
                    taken(0, b_pTa)
                    taken(1, b_pTb)
                if lo <= 3 <= hi:
                    wait(act, b_lmax, t - 2)
                    act.activation(gt[:, o, :], ps[:, 7, 0:EXPERTS], ACT.Exp, bias=nlm[:, o:o + 1],
                                   accum_out=gsum[:, o:o + 1]).then_inc(b_lexp, 1)
                if lo <= 1 <= hi:
                    taken(2, b_pTc)
                    taken(3, b_pTd)
                if lo <= 0 <= hi:
                    wait(act, b_max, t + 1)
                    wait(act, b_pTp, 4 * (t - 1))
                    for half, (c0, c1) in enumerate(((0, 2 * BANK), (2 * BANK, KEYS))):
                        act.activation(pe2[:, p, c0:c1], ps[:, 0:4, :].rearrange("p a b -> p (a b)")[:, c0:c1], ACT.Exp,
                                       bias=nmx[:, p:p + 1], accum_out=sm2[:, r % 4, half:half + 1]).then_inc(b_exp, 1)

            crossing(attend, period)
            tiles(act, period, first=1)

            def silu3(c):
                for j in range(FCH):
                    act.wait_ge(d_gate, 3 * c + j + 1)
                    if not (isinstance(c, int) and c == 0):
                        act.wait_ge(d_g, 3 * c - FCH + j + 1)
                    act.activation(sil3[:, j, :], ps[:, 3 + j, :], ACT.Silu).then_inc(d_sil, 1)

            silu3(0)
            with act.Fori(1, TOKENS // BANK) as c:
                silu3(c)

            def step(e, i, k, lo, hi):
                p = i % 2
                if lo <= 0 <= hi:
                    act.wait_ge(e_h, 2 * e + 1)
                    act.activation(sil4[:, p, :], ps[:, 3 + p, 0:FCH * CAP], ACT.Silu).then_inc(e_sil, 1)
                if lo <= -1 <= hi:
                    act.wait_ge(e_xTp, e + 2)
                    act.activation(xeT[:, 1 - p, :], ps[:, 0, 0:CAP], ACT.Copy).then_inc(e_xT, 1)
                if lo <= 1 <= hi:
                    act.wait_ge(e_yTp, e)
                    if not (isinstance(e, int) and e < 3):
                        act.wait_ge(e_yp, e - 2)
                    act.activation(yT[:, 1 - p, :], ps[:, 5, 0:CAP], ACT.Copy).then_inc(e_yT, 1)

            periods(act, step, EXPERTS, 1, 2)

        @block.vector
        def _(dve):
            def attend(b, r, k, lo, hi):
                p, o = r % 2, 1 - r % 2
                ln1, ln2 = Chain(dve, a_c1, b + 2, 2), Chain(dve, a_c2, b - 4, 2)
                if isinstance(b, int) and b == 0:
                    dve.tensor_copy(tri[:, :], C[:, C_TRI:C_TRI + P])
                    dve.tensor_scalar(chosen[:, :], ident, float(CHOSEN), None, ALU.mult).then_inc(s_ready, 1)
                if lo <= -2:
                    if isinstance(b, int) and b in (0, STEP - 1):
                        dve.wait_ge(s_x1 if b == 0 else s_x2, 16)
                    for i in range(2):
                        last = dve.bn_stats(st1[:, 2 * p + i, :], tile_of(2 * (b + 2) + i))
                    n_st1 = ln1.mark(last)

                def rotated(w):
                    cols = slice(w * SEQ, (w + 1) * SEQ)
                    dve.wait_ge(a_qkp, 2 * b + w + 1)
                    if w == 0:
                        wait(dve, a_qk, b - 1)
                    for i, (dst, tab) in enumerate(((rc, C_COS), (rsn, C_SIN))):
                        last = dve.scalar_tensor_tensor(dst[:, p, cols], ps[:, w, i * SEQ:(i + 1) * SEQ],
                                                        bias[:, 2 * w + i:2 * w + i + 1],
                                                        C[:, tab + w * SEQ:tab + (w + 1) * SEQ], ALU.add, ALU.mult)
                    last.then_inc(a_rope, 1)

                if isinstance(b, int) and b == 0:
                    dve.wait_ge(s_rot, 16)
                if lo <= 0 <= hi:
                    rotated(0)
                if lo <= -2:
                    ln1.need(n_st1, s_x0)
                    for i in range(2):
                        last = dve.bn_aggr(mv1[:, 2 * p + i, :], st1[:, 2 * p + i, :])
                    n_mv1 = ln1.mark(last)
                if lo <= 0 <= hi:
                    rotated(1)
                if lo <= 4 <= hi:
                    if r == 0:
                        dve.wait_ge(a_norm2, k)
                    dve.wait_ge(a_outp, b - 3)
                    dve.wait_ge(a_x, b - 3)
                    dve.wait_ge(a_ri, b - 3)
                    for i in range(2):
                        xb = tile_of(2 * (b - 4) + i)
                        last = dve.scalar_tensor_tensor(xb, ps[:, 6, i * P:(i + 1) * P], ri1[:, r, i:i + 1], xb,
                                                        ALU.mult, ALU.add)
                    last.then_inc(a_x1, 1)
                if lo <= -2:
                    ln1.need(n_mv1)
                    wait(dve, a_rstd, b + 1)
                    dve.tensor_scalar(ng1[:, 2 * p:2 * p + 2], mv1[:, 2 * p:2 * p + 2, 0], -1.0, None, ALU.mult)
                    dve.tensor_scalar(vv1[:, 2 * p:2 * p + 2], mv1[:, 2 * p:2 * p + 2, 1], EPS, None, ALU.add)\
                        .then_inc(a_stats, 1)
                if isinstance(b, int) and b == -2:
                    dve.wait_ge(s_attn, 4 * 16)
                    dve.tensor_copy(bv_all[:, :], bias[:, 4:5].to_broadcast([P, P])).then_inc(s_bvw, 1)
                    dve.tensor_copy(maskb[:, :], C[:, C_MASK:C_MASK + P])
                    dve.tensor_copy(identb[:, :], ident).then_inc(s_ready, 1)
                    dve.wait_ge(s_bvw, 2)
                    dve.tensor_tensor(bo_all[:, :], bo_all[:, :], ps[:, 6, 0:DIM], ALU.add).then_inc(s_bvw, 1)
                if lo <= 4 <= hi:
                    wait_apart(dve, s_x0, a_x1, b - 3)
                    for i in range(2):
                        last = dve.bn_stats(st2[:, 2 * r + i, :], tile_of(2 * (b - 4) + i))
                    ln2.mark(last)
                if lo <= 1 <= hi:
                    dve.wait_ge(a_sc, b)
                    wait(dve, a_exp, b - 2)
                    dve.tensor_reduce(nm1[:, o, 0:1], ps[:, 3, 0:P], AX.X, ALU.max, negate=True)
                    dve.tensor_reduce(nm1[:, o, 1:2], ps[:, 3, P:3 * P], AX.X, ALU.max, negate=True)\
                        .then_inc(a_max, 1)
                if lo <= 4 <= hi:
                    ln2.need(ln2.n, s_x0)
                    for i in range(2):
                        last = dve.bn_aggr(mv2[:, 2 * r + i, :], st2[:, 2 * r + i, :])
                    ln2.mark(last)
                if lo <= 2 <= hi:
                    dve.wait_ge(a_exp, b - 1)
                    dve.reciprocal(ri1[:, (r + 2) % STEP, :], sm1[:, (r + 2) % STEP, :]).then_inc(a_ri, 1)
                if lo <= 4 <= hi:
                    ln2.need(ln2.n)
                    dve.tensor_scalar(vv2[:, 2 * r:2 * r + 2], mv2[:, 2 * r:2 * r + 2, 1], EPS, None, ALU.add)\
                        .then_inc(a_stats2, 1)

            dve.wait_ge(s_x0, 16)
            dve.wait_ge(s_poolc, 2)
            periods(dve, attend, BATCHES, 2, 4, end=BATCHES + 2)

            def mul3(c, p, j):
                dve.wait_ge(d_sil, 3 * c + j + 1)
                dve.wait_ge(d_up, 3 * c + j + 1)
                if not (isinstance(c, int) and c < 2):
                    dve.wait_ge(d_y, c - 1)
                dve.tensor_tensor(g3[:, p, j, :], sil3[:, j, :], ps[:, j, :], ALU.mult).then_inc(d_g, 1)

            def period(t, r, floor, lo, hi):
                p, o = r % 2, 1 - r % 2
                now, last, prev, third, fourth = (lo <= lag <= hi for lag in range(5))
                x3, rt, sl, mc = Chain(dve, c_x3, t - 2, 12), Chain(dve, c_rt, t - 3, 5), \
                    Chain(dve, c_sl, t - 4, 2), Chain(dve, c_mx, t, 2)
                row2, row3, row4 = ((r - lag) % RING for lag in (2, 3, 4))
                v, vh, a, y = (buf[:, p:p + 1] for buf in (vv3, vh3, ra3, rs3))
                flat = ps[:, 0:4, :].rearrange("p a b -> p (a b)")

                def newton_a():
                    x3.need(x3.n)
                    x3.mark(dve.scalar_tensor_tensor(a, y, vh, y, ALU.mult, ALU.mult))

                def newton_y():
                    x3.need(x3.n)
                    x3.mark(dve.scalar_tensor_tensor(y, a, 1.5, y, ALU.add, ALU.mult))

                if isinstance(t, int) and t == TILES + 3:
                    mul3(0, 0, 0)
                    mul3(0, 0, 1)
                if fourth:
                    wait(dve, b_rank, t - 3)
                    dve.tensor_scalar(over[:, :], ps[:, 7, 0:EXPERTS], float(CHOSEN + CAP), FAR, ALU.is_ge, ALU.mult)
                    dve.tensor_tensor(slot[:, :], ps[:, 7, 0:EXPERTS], C[:, C_BASE:C_BASE + EXPERTS], ALU.add)\
                        .then_inc(b_rkd, 1)
                if prev:
                    wait(dve, b_pv, t - 1)
                    dve.scalar_tensor_tensor(tile_of(t - 2), ps[:, 6, 0:DIM], ri2[:, p:p + 1], tile_of(t - 2),
                                             ALU.mult, ALU.add).then_inc(b_x2, 1)
                if fourth:
                    wait(dve, b_rkd, t - 3)
                    sl.mark(dve.tensor_tensor(slot[:, :], slot[:, :], over[:, :], ALU.add))
                if prev:
                    wait_apart(dve, s_ready, b_x2, t - 1)
                    x3.mark(dve.bn_stats(st3[:, p, :], tile_of(t - 2)))
                if fourth:
                    sl.need(sl.n, s_ready)
                    sl.mark(dve.max(slot8[:, :], slot[:, :]))
                if prev:
                    x3.need(x3.n, s_ready)
                    x3.mark(dve.bn_aggr(mv3[:, p, :], st3[:, p, :]))
                if fourth:
                    sl.need(sl.n)
                    dve.tensor_scalar(idx[:, row4, :], slot8[:, :], -1.0 - CHOSEN, None, ALU.add).then_inc(b_idx, 1)
                if last:
                    wait(dve, b_exp, 2 * t)
                    row = sm2[:, (r - 1) % 4, :]
                    dve.tensor_tensor(all2[:, o:o + 1], row[:, 0:1], row[:, 1:2], ALU.add).then_inc(b_sum, 1)
                if prev:
                    x3.need(x3.n)
                    x3.mark(dve.tensor_scalar(v, mv3[:, p, 1:2], EPS, None, ALU.add))
                if last:
                    wait(dve, b_sum, t)
                    dve.reciprocal(ri2[:, o:o + 1], all2[:, o:o + 1]).then_inc(b_ri, 1)
                if prev:
                    x3.need(x3.n)
                    n_y = x3.mark(dve.tensor_scalar(y.bitcast(I32), v.bitcast(I32), 1, None, ALU.logical_shift_right))
                    x3.mark(dve.tensor_scalar(vh, v, -0.5, None, ALU.mult))
                    x3.need(n_y)
                    x3.mark(dve.tensor_scalar(y.bitcast(I32), y.bitcast(I32), -1.0, float(0x5F3759DF),
                                              ALU.mult, ALU.add))
                    wait(dve, b_scat[row2], 16 * (TOPK * floor(2, RING) + 1))
                    tok = rows[:, row2, ROW - 1:ROW].bitcast(I32)
                    dve.tensor_scalar(tok, tok, float(RING * P), None, ALU.add)
                if now:
                    wait(dve, b_sc, 2 * t + 1)
                    mc.mark(dve.tensor_reduce(mx[:, p, 0:1], flat[:, 0:2 * BANK], AX.X, ALU.max))
                if prev:
                    newton_a()
                if third:
                    wait(dve, b_lg, t - 2)
                    dve.tensor_reduce(nlm[:, o:o + 1], ps[:, 7, 0:EXPERTS], AX.X, ALU.max, negate=True)\
                        .then_inc(b_lmax, 1)
                if prev:
                    newton_y()
                    newton_a()
                    newton_y()
                if third:
                    wait_apart(dve, s_ready, b_lexp, t - 2)
                    n_top = rt.mark(dve.max(top[:, o, :], gt[:, o, :]))
                if prev:
                    newton_a()
                if third:
                    rt.need(n_top, s_ready)
                    n_left = rt.mark(dve.match_replace(left[:, o, :], top[:, o, :], gt[:, o, :], -1.0))
                if prev:
                    newton_y()
                if now:
                    wait(dve, b_sc, 2 * t + 2)
                    n_max = mc.mark(dve.tensor_reduce(mx[:, p, 1:2], flat[:, 2 * BANK:KEYS], AX.X, ALU.max))
                if third:
                    rt.need(n_left)
                    n_mask = rt.mark(dve.tensor_scalar(mask[:, o, :], left[:, o, :], 0.0, None, ALU.is_lt))
                if now:
                    mc.need(n_max)
                    dve.tensor_reduce(nmx[:, p:p + 1], mx[:, p, 0:2], AX.X, ALU.max, negate=True).then_inc(b_max, 1)
                if prev:
                    x3.need(x3.n)
                    dve.tensor_scalar(rows[:, row2, 0:DIM], tile_of(t - 2), mv3[:, p, 0:1], y,
                                      ALU.subtract, ALU.mult).then_inc(b_x3n, 1)
                if third:
                    rt.need(n_mask)
                    wait(dve, b_rank, t - 3)
                    wait(dve, b_mask, t - 3)
                    dve.tensor_tensor(before[:, p, :], before[:, o, :], mask[:, o, :], ALU.add).then_inc(b_mask, 1)
                    n_sum = rt.mark(dve.tensor_reduce(tsum[:, o:o + 1], top[:, o, :], AX.X, ALU.add))
                if third:
                    rt.need(n_sum)
                    rt(dve.scalar_tensor_tensor(tsum[:, o:o + 1], gsum[:, o:o + 1], FLOAT_EPS,
                                                tsum[:, o:o + 1], ALU.mult, ALU.max))
                    dve.reciprocal(tsum[:, o:o + 1], tsum[:, o:o + 1]).then_inc(b_wsum, 1)
                    wait(dve, b_wsum, t - 2)
                    dve.tensor_scalar(rows[:, row3, DIM:DIM + EXPERTS], gt[:, o, :], tsum[:, o:o + 1], None, ALU.mult)

            crossing(attend, period)
            tiles(dve, period, first=1)

            def muls(c, p):
                for j in range(FCH):
                    mul3(c, p, j)

            def sum3(c, p):
                dve.wait_ge(d_y, c + 1)
                if not (isinstance(c, int) and c < 2):
                    dve.wait_ge(d_st[p], 16 * (c // 2))
                dve.tensor_tensor(o3[:, p, :, :].rearrange("p a c -> p (a c)"), ps[:, 6 + p, :],
                                  X[:, bass.ds(4 * c, 4), :].rearrange("p a c -> p (a c)"), ALU.add).then_inc(d_o, 1)

            mul3(0, 0, 2)
            muls(1, 1)
            sum3(0, 0)
            def two3(k):
                for p in range(2):
                    muls(2 * k + p, p)
                    c = 2 * k + p - 1
                    dve.wait_ge(d_y, c + 1)
                    wait(dve, d_st[1 - p], 16 * (k - 1 + p))
                    dve.tensor_tensor(o3[:, 1 - p, :, :].rearrange("p a c -> p (a c)"), ps[:, 7 - p, :],
                                      X[:, bass.ds(4 * c, 4), :].rearrange("p a c -> p (a c)"), ALU.add)\
                        .then_inc(d_o, 1)

            two3(1)
            with dve.Fori(2, TOKENS // BANK // 2) as k:
                two3(k)
            sum3(TOKENS // BANK - 1, 1)

            def step(e, i, k, lo, hi):
                p = i % 2
                if lo <= 0 <= hi:
                    dve.wait_ge(e_sil, e + 1)
                    dve.wait_ge(e_h, 2 * e + 2)
                    if not (isinstance(e, int) and e < 2):
                        dve.wait_ge(e_yTp, e - 1)
                    dve.tensor_tensor(g4[:, p, :], sil4[:, p, :], ps[:, 1 + p, 0:FCH * CAP], ALU.mult).then_inc(e_g, 1)
                if lo <= 2 <= hi:
                    i2 = (i + 2) % STEP
                    dve.wait_ge(e_yp, e - 1)
                    dve.wait_ge(e_row, e - 1)
                    gate = gate4[:, i2, :].unsqueeze(2).to_broadcast([HALF, 2, DIM])
                    dve.tensor_tensor(yr[:, i2, :, :], ps[0:HALF, 6, 0:2 * DIM].rearrange("p (h c) -> p h c", h=2),
                                      gate, ALU.mult).then_inc(e_y, 1)
                if lo <= 0 <= hi:
                    if not (isinstance(e, int) and e < STEP):
                        dve.wait_ge(e_add[p], 32 * (2 * k + i // 2 - 1))
                    dve.wait_ge(r_in[i], 16 * (k + 1))
                    dve.tensor_copy(tok4[:, i, :], er[:, i, :, ROW - 1])
                    dve.tensor_copy(gate4[:, i, :], er[:, i, :, bass.ds(e + DIM, 1)].rearrange("p h a -> p (h a)"))\
                        .then_inc(e_row, 1)

            periods(dve, step, EXPERTS, 1, 2)


def periods(eng, period, items, ahead, behind, first=None, end=None):
    def bounds(t):
        return max(-ahead, t - items + 1), min(t, behind)

    for t in range(-ahead if first is None else first, STEP):
        period(t, t % STEP, t // STEP, *bounds(t))
    with eng.Fori(1, items // STEP - 1) as k:
        for r in range(STEP):
            period(k * STEP + r, r, k, -ahead, behind)
    for t in range(items - STEP, items + behind if end is None else end):
        period(t, t % STEP, t // STEP, *bounds(t))


def crossing(attend, period):
    def cross(t):
        period(t, t % RING, lambda lag, n: (t - lag) // n, -2, t)

    def attend_last(b):
        attend(b, b % STEP, b // STEP, b - BATCHES + 1, 4)

    cross(-2)
    cross(-1)
    attend_last(BATCHES + 2)
    cross(0)
    attend_last(BATCHES + 3)


def tiles(eng, period, first=-2):
    def peeled(t):
        period(t, t % RING, lambda lag, n: (t - lag) // n, max(-2, t - TILES + 1), min(t, 4))

    start, turns = 4, (TILES - 5) // RING
    for t in range(first, start):
        peeled(t)
    with eng.Fori(0, turns) as k:
        for i in range(RING):
            period(k * RING + start + i, (start + i) % RING,
                   lambda lag, n, i=i: k * (RING // n) + (start + i - lag) // n, -2, 4)
    for t in range(start + turns * RING, TILES + 4):
        peeled(t)


def kernel(x, ctx_1024, L0_attn_Wq, L0_attn_bq, L0_attn_Wk, L0_attn_bk, L0_attn_Wv, L0_attn_bv, L0_attn_Wo,
           L0_attn_bo, L0_xattn_prefix_k, L0_xattn_prefix_v, L0_ffn_wg, L0_ffn_shared_w1, L0_ffn_shared_w2,
           L0_ffn_expert_w1, L0_ffn_expert_w2):
    import concourse.bacc as bacc
    from concourse.bass_utils import run_bass_kernel_spmd

    def lay(a):
        return np.ascontiguousarray(a)

    def packed(w1, w2):
        lead = w1.shape[:-2]
        a = np.swapaxes(w1, -1, -2)
        b = np.swapaxes(w2, -1, -2).reshape(*lead, FCH, P, DIM)
        b = np.moveaxis(b, -3, -2).reshape(*lead, P, FCH * DIM)
        return lay(np.concatenate([a, b], axis=-1))

    swap = np.arange(DIM) ^ 1
    x, ctx = np.asarray(x), np.asarray(ctx_1024)
    Wq, Wk, Wv, Wo = (np.asarray(w) for w in (L0_attn_Wq, L0_attn_Wk, L0_attn_Wv, L0_attn_Wo))
    bq, bk, bv, bo = (np.asarray(w) for w in (L0_attn_bq, L0_attn_bk, L0_attn_bv, L0_attn_bo))
    arrays = {
        "x": lay(x.reshape(TOKENS, DIM)),
        "ctxT": lay(ctx.transpose(0, 2, 1)),
        "ctxN": lay(ctx),
        "preT": lay(np.asarray(L0_xattn_prefix_k).T),
        "preV": lay(np.asarray(L0_xattn_prefix_v)),
        "wqkvo": lay(np.stack([Wq, Wq[:, swap], Wk, Wk[:, swap], Wv, Wo], axis=1)),
        "bcol": lay(np.stack([bq, bq[swap], bk, bk[swap], bv], axis=1)),
        "bo": lay(bo.reshape(1, DIM)),
        "wgT": lay(np.asarray(L0_ffn_wg).T),
        "sw": packed(np.asarray(L0_ffn_shared_w1), np.asarray(L0_ffn_shared_w2)),
        "ew": packed(np.asarray(L0_ffn_expert_w1), np.asarray(L0_ffn_expert_w2)),
        "cst": constants(),
    }
    nc = bacc.Bacc("TRN2", target_bir_lowering=False, num_devices=1)
    args = [nc.dram_tensor(n, a.shape, mybir.dt.from_np(a.dtype), kind="ExternalInput").ap() for n, a in arrays.items()]
    out = nc.dram_tensor("out", [TOKENS + SPARE, DIM], F32, kind="ExternalOutput").ap()
    decoder_layer(nc, *args, out)
    r = run_bass_kernel_spmd(nc, [arrays], core_ids=[0])
    return r.results[0]["out"][0:TOKENS].reshape(BATCHES, SEQ, DIM)
```
